# Optimizing a Trainium2 kernel written in Bass

```python
import numpy as np
import jax
import jax.numpy as jnp

def _softmax(x, axis=-1):
    return jax.nn.softmax(x, axis=axis)

def _gelu(x):
    return jax.nn.gelu(x, approximate=True)

def _silu(x):
    return jax.nn.silu(x)

def _sigmoid(x):
    return jax.nn.sigmoid(x)

def _layernorm(x, axis=-1, eps=1e-05):
    m = jnp.mean(x, axis=axis, keepdims=True)
    v = jnp.var(x, axis=axis, keepdims=True)
    return (x - m) / jnp.sqrt(v + eps)

def _scatter_add(tgt, idx, src, axis=0):
    return tgt.at[idx].add(src)

def _segment_sum(src, seg, n):
    return jax.ops.segment_sum(src, seg, n)
kernel_name = 'mk_adj_preln_d2_adj_r2_88e37d'

def setup_inputs(seed: int=0):
    np.random.seed(seed)
    _w = jnp.asarray

    def _rec_inputs():
        import jax
        import jax.numpy as jnp
        _gk = jax.random.key(seed)
        x = -1.394e-06 + 0.9999 * jax.random.normal(jax.random.fold_in(_gk, 1), (2048, 256), jnp.float32)
        _a = jax.random.bernoulli(jax.random.fold_in(_gk, 2), 0.00195312, (2048, 2048))
        adj = _a.astype(jnp.int32)
        _nm = jnp.ones((2048,), dtype=bool)
        nodemask = jnp.where(_nm, 1.0, 0.0).astype(jnp.int32)
        return (x, adj, nodemask)
    x, adj, nodemask = _rec_inputs()

    def _L0_gnn_setup():
        import jax, jax.numpy as jnp
        import numpy as np
        N = 4096
        IN_F = 256
        OUT_F = 256
        ALPHA = 0.2
        NEG_BIG = -9000000000000000.0
        key = jax.random.key(seed)
        k1, k2, k3, k4 = jax.random.split(key, 4)
        adjacency = jax.random.randint(k1, (N, N), 0, 2, dtype=jnp.int32)
        features = jax.random.normal(k2, (N, IN_F), dtype=jnp.float32)
        W = jax.random.normal(k3, (IN_F, OUT_F), dtype=jnp.float32) * (1.0 / np.sqrt(IN_F))
        attn = jax.random.normal(k4, (2 * OUT_F, 1), dtype=jnp.float32) * 0.05
        return {'adjacency': adjacency, 'features': features, 'W': W, 'attn': attn}
    _L0_gnn_all = _L0_gnn_setup()
    _L0_gnn_in = {k: v for k, v in _L0_gnn_all.items() if k in ('W', 'attn')}
    del _L0_gnn_all

    def _L1_gnn_setup():
        import jax, jax.numpy as jnp
        import numpy as np
        D = 256
        H = 8
        HD = D // H
        EPS = 1e-05
        NEG = -1e+30

        def layer_norm(x, scale, bias):
            mu = jnp.mean(x, axis=-1, keepdims=True)
            var = jnp.mean(jnp.square(x - mu), axis=-1, keepdims=True)
            return (x - mu) * jax.lax.rsqrt(var + EPS) * scale + bias
        key = jax.random.key(seed)
        ks = jax.random.split(key, 16)
        S = T = 2048
        inp = {'h_source': jax.random.normal(ks[0], (S, D), jnp.float32), 'h_target': jax.random.normal(ks[1], (T, D), jnp.float32), 'edge_mask': jax.random.randint(ks[2], (T, S), 0, 2, jnp.int32), 'source_mask': jnp.ones((S,), jnp.int32), 'target_mask': jnp.ones((T,), jnp.int32), 'ln1_scale': jnp.ones((D,), jnp.float32), 'ln1_bias': jnp.zeros((D,), jnp.float32), 'Wq': jax.random.normal(ks[3], (D, D), jnp.float32) / np.sqrt(D), 'bq': jnp.zeros((D,), jnp.float32), 'Wk': jax.random.normal(ks[4], (D, D), jnp.float32) / np.sqrt(D), 'bk': jnp.zeros((D,), jnp.float32), 'Wv': jax.random.normal(ks[5], (D, D), jnp.float32) / np.sqrt(D), 'bv': jnp.zeros((D,), jnp.float32), 'Wo': jax.random.normal(ks[6], (D, D), jnp.float32) / np.sqrt(D), 'bo': jnp.zeros((D,), jnp.float32), 'ln2_scale': jnp.ones((D,), jnp.float32), 'ln2_bias': jnp.zeros((D,), jnp.float32), 'W1': jax.random.normal(ks[7], (D, 4 * D), jnp.float32) / np.sqrt(D), 'W2': jax.random.normal(ks[8], (4 * D, D), jnp.float32) / np.sqrt(4 * D)}
        return inp
    _L1_gnn_all = _L1_gnn_setup()
    _L1_gnn_in = {k: v for k, v in _L1_gnn_all.items() if k in ('h_target', 'ln1_scale', 'ln1_bias', 'Wq', 'bq', 'Wk', 'bk', 'Wv', 'bv', 'Wo', 'bo', 'ln2_scale', 'ln2_bias', 'W1', 'W2')}
    del _L1_gnn_all
    return {'x': x, 'adj': adj, 'nodemask': nodemask, 'L0_gnn_W': _L0_gnn_in['W'], 'L0_gnn_attn': _L0_gnn_in['attn'], 'L1_gnn_h_target': _L1_gnn_in['h_target'], 'L1_gnn_ln1_scale': _L1_gnn_in['ln1_scale'], 'L1_gnn_ln1_bias': _L1_gnn_in['ln1_bias'], 'L1_gnn_Wq': _L1_gnn_in['Wq'], 'L1_gnn_bq': _L1_gnn_in['bq'], 'L1_gnn_Wk': _L1_gnn_in['Wk'], 'L1_gnn_bk': _L1_gnn_in['bk'], 'L1_gnn_Wv': _L1_gnn_in['Wv'], 'L1_gnn_bv': _L1_gnn_in['bv'], 'L1_gnn_Wo': _L1_gnn_in['Wo'], 'L1_gnn_bo': _L1_gnn_in['bo'], 'L1_gnn_ln2_scale': _L1_gnn_in['ln2_scale'], 'L1_gnn_ln2_bias': _L1_gnn_in['ln2_bias'], 'L1_gnn_W1': _L1_gnn_in['W1'], 'L1_gnn_W2': _L1_gnn_in['W2']}

def reference(x, adj, nodemask, L0_gnn_W, L0_gnn_attn, L1_gnn_h_target, L1_gnn_ln1_scale, L1_gnn_ln1_bias, L1_gnn_Wq, L1_gnn_bq, L1_gnn_Wk, L1_gnn_bk, L1_gnn_Wv, L1_gnn_bv, L1_gnn_Wo, L1_gnn_bo, L1_gnn_ln2_scale, L1_gnn_ln2_bias, L1_gnn_W1, L1_gnn_W2):
    import jax
    import jax.numpy as jnp

    def _L0_gnn_ref(adjacency, features, W, attn):
        import jax, jax.numpy as jnp
        import numpy as np
        N = 4096
        IN_F = 256
        OUT_F = 256
        ALPHA = 0.2
        NEG_BIG = -9000000000000000.0
        h = features @ W
        a1 = attn[:OUT_F, 0]
        a2 = attn[OUT_F:, 0]
        s1 = h @ a1
        s2 = h @ a2
        e = jax.nn.leaky_relu(s1[:, None] + s2[None, :], negative_slope=ALPHA)
        e = jnp.where(adjacency > 0, e, NEG_BIG)
        attention = jax.nn.softmax(e, axis=1)
        h_prime = attention @ h
        return jax.nn.elu(h_prime)

    def _L1_gnn_ref(h_source, h_target, edge_mask, source_mask, target_mask, ln1_scale, ln1_bias, Wq, bq, Wk, bk, Wv, bv, Wo, bo, ln2_scale, ln2_bias, W1, W2):
        import jax, jax.numpy as jnp
        import numpy as np
        D = 256
        H = 8
        HD = D // H
        EPS = 1e-05
        NEG = -1e+30

        def layer_norm(x, scale, bias):
            mu = jnp.mean(x, axis=-1, keepdims=True)
            var = jnp.mean(jnp.square(x - mu), axis=-1, keepdims=True)
            return (x - mu) * jax.lax.rsqrt(var + EPS) * scale + bias
        smask = (source_mask == 1)[:, None]
        tmask = (target_mask == 1)[:, None]
        hs = layer_norm(h_source, ln1_scale, ln1_bias)
        ht = layer_norm(h_target, ln1_scale, ln1_bias)
        hs = jnp.where(smask, hs, 0.0)
        ht = jnp.where(tmask, ht, 0.0)
        T, S = (ht.shape[0], hs.shape[0])
        q = (ht @ Wq + bq).reshape(T, H, HD) / jnp.sqrt(jnp.float32(HD))
        k = (hs @ Wk + bk).reshape(S, H, HD)
        v = (hs @ Wv + bv).reshape(S, H, HD)
        logits = jnp.einsum('thd,shd->hts', q, k)
        logits = jnp.where(edge_mask[None] != 0, logits, NEG)
        probs = jax.nn.softmax(logits, axis=-1)
        ctx = jnp.einsum('hts,shd->thd', probs, v).reshape(T, D)
        attn = ctx @ Wo + bo
        attn = jnp.where(tmask, attn, 0.0)
        ht = ht + attn
        ht = layer_norm(ht, ln2_scale, ln2_bias)
        ht = jnp.where(tmask, ht, 0.0)
        ff = jax.nn.gelu(ht @ W1) @ W2
        return ht + ff
    h = jnp.maximum(_layernorm(x, axis=-1), 0.0)
    x = x + _L0_gnn_ref(adj, h, L0_gnn_W, L0_gnn_attn)
    h = jnp.maximum(_layernorm(x, axis=-1), 0.0)
    x = x + _L1_gnn_ref(h, L1_gnn_h_target, adj, nodemask, nodemask, L1_gnn_ln1_scale, L1_gnn_ln1_bias, L1_gnn_Wq, L1_gnn_bq, L1_gnn_Wk, L1_gnn_bk, L1_gnn_Wv, L1_gnn_bv, L1_gnn_Wo, L1_gnn_bo, L1_gnn_ln2_scale, L1_gnn_ln2_bias, L1_gnn_W1, L1_gnn_W2)
    return x

_drawn_inputs = setup_inputs


def setup_inputs(seed=0):
    import zlib

    import numpy as np

    out = dict(_drawn_inputs(seed))
    spreads = {'L1_gnn_ln1_scale': (1.0, 0.2),
     'L1_gnn_ln1_bias': (0.0, 0.1),
     'L1_gnn_bq': (0.0, 0.455),
     'L1_gnn_bk': (0.0, 0.8),
     'L1_gnn_bv': (0.0, 0.1),
     'L1_gnn_bo': (0.0, 0.1),
     'L1_gnn_ln2_scale': (1.0, 0.2),
     'L1_gnn_ln2_bias': (0.0, 0.1)}
    factors = {}
    for name, (base, spread) in spreads.items():
        noise = np.random.default_rng([zlib.crc32(name.encode()), seed]).standard_normal(out[name].shape)
        drawn = base * np.exp(spread * noise) if base else spread * noise
        out[name] = jnp.asarray(drawn.astype(out[name].dtype))
    for name, factor in factors.items():
        out[name] = (out[name] * factor).astype(out[name].dtype)
    return out
```

```python
from contextlib import ExitStack

import concourse.bass as bass
from concourse import mybir

ALU = mybir.AluOpType
ACT = mybir.ActivationFunctionType
F32 = mybir.dt.float32
F32R = mybir.dt.float32r
BF16 = mybir.dt.bfloat16
I32 = mybir.dt.int32

P = 128
N = 2048
D = 256
KC = D // P
NT = N // P
HEADS = 8
HD = D // HEADS
HPC = P // HD
HID = 4 * D
MC = HID // P
CH = 4
BLK = N // CH // P
HALF = N // 2
UNITS = NT * HEADS
GT = 4
NG = NT // GT
EPS = 1e-5
ALPHA = 0.2
MASKED = -float(2 ** 100)
LOWEST = -3.0e38
QSCALE = HD ** -0.5


class Tile:

    def __init__(self, t=None, pair=None, parity=None):
        if isinstance(t, int):
            self.t, self.parity, self.pair = t, t % 2, t // 2
        else:
            self.parity, self.pair = parity, pair
            self.t = pair * 2 + parity
        self.static = isinstance(t, int)

    def ahead(self, k):
        if self.static:
            return Tile(self.t + k)
        n = self.parity + k
        return Tile(pair=self.pair + n // 2, parity=n % 2)

    def real(self):
        return not self.static or 0 <= self.t < NT


def tile_loop(eng, step, lead):
    for t in range(-lead, 2):
        step(Tile(t))
    with eng.Fori(1, NT // 2 - 1) as pair:
        for parity in range(2):
            step(Tile(pair=pair, parity=parity))
    for t in (NT - 2, NT - 1):
        step(Tile(t))


class Chain:

    def __init__(self, eng, sem, start):
        self.eng, self.sem, self.start, self.n = eng, sem, start, 0

    def link(self, ins, apart=None):
        self.n += 1
        ins.then_inc(self.sem, 1)
        if apart:
            apart(self.eng, (self.sem, self.start + self.n))
        else:
            self.eng.wait_ge(self.sem, self.start + self.n)


def build(nc, x, adj, nodemask, W0, attn0, h_target, ln1_scale, ln1_bias, Wq, bq, Wk, bk, Wv, bv, Wo, bo,
          ln2_scale, ln2_bias, W1, W2, out):
    ctx = ExitStack()
    with ctx:
        def sb(name, shape, dt=F32):
            return ctx.enter_context(nc.sbuf_tensor(name, shape, dt))

        def ps(name, shape):
            return ctx.enter_context(nc.psum_tensor(name, shape, F32))

        def sem(name):
            return ctx.enter_context(nc.semaphore(name))

        key_dram = nc.dram_tensor("key_split", (2, D, N), F32).ap()
        query_dram = nc.dram_tensor("query_split", (2, D, N), F32).ap()
        target_dram = nc.dram_tensor("target_normed", (N, D), F32).ap()

        key_stack = sb("key_stack", [P, HEADS, N], F32R)
        value = sb("value", [P, NT, HEADS, HD + 1])
        xres = sb("xres", [P, NT, D])
        hproj = sb("hproj", [P, NT, D + 1])
        context = hproj[:, :, 0:D]
        ring = sb("ring", [P, 4, N])
        src_row = ring[:, 2, :]
        w0 = ring[:, 3, 0:KC * D].rearrange("p (c n) -> p c n", c=KC)
        att = ring[:, 3, KC * D:KC * D + 2 * D].rearrange("p (c n) -> p c n", c=2)
        w1 = ring[:, 0, :].rearrange("p (c n) -> p c n", c=KC)
        w2 = ring[:, 1, :].rearrange("p (c n) -> p c n", c=MC)
        probsT = sb("probsT", [P, CH, BLK * P])
        spare = sb("spare", [P, N])
        adj_in = spare[:, :].bitcast(I32)
        mask = sb("mask", [P, 2, N], BF16)
        query_stack = sb("query_stack", [P, 2, HEADS, P], F32R)
        wq, wk, wv, wo = (sb(n, [P, KC, D]) for n in ("wq", "wk", "wv", "wo"))
        ln1s, ln1b, ln2s, ln2b, bvr, bor = (sb(n, [P, D]) for n in ("ln1s", "ln1b", "ln2s", "ln2b", "bvr", "bor"))
        bqc, bkc = sb("bqc", [P, KC]), sb("bkc", [P, KC])
        node_i, node = sb("node_i", [P, NT], I32), sb("node", [P, NT])
        ident = sb("ident", [P, P])
        s1 = sb("s1", [P, NT])
        s2 = sb("s2", [P, 2])
        minus_half = sb("minus_half", [P, 1])
        stats, mv, rstd = sb("stats", [P, 6]), sb("mv", [P, 2]), sb("rstd", [P, 1])
        normed = sb("normed", [P, 2, D])
        normedT = sb("normedT", [P, 2, KC, P])
        row1, row2, row3 = sb("row1", [P, D]), sb("row2", [P, D]), sb("row3", [P, D])
        rowmax, negmax = sb("rowmax", [P, 4, 2]), sb("negmax", [P, 4])
        recip = sb("recip", [P, HEADS])
        whole = sb("whole", [P, KC, P])
        part_a, part_b = sb("part_a", [P, KC, P], F32R), sb("part_b", [P, KC, P], F32R)
        affine = sb("affine", [P, D])
        target_in = sb("target_in", [P, 2, D])
        hiddenT = ring[:, 2:4, :].rearrange("p a (m n) -> p (a m) n", n=GT * P)
        postT = probsT[:, 0:2, :]
        post = probsT[:, 2:4, :].rearrange("p a (k n) -> p (a k) n", n=D)
        ctx_rows = spare[:, 0:GT * D].rearrange("p (k n) -> p k n", n=D)
        target_rows = spare[:, GT * D:2 * GT * D].rearrange("p (k n) -> p k n", n=D)

        pq = ps("pq", [P, 2, HALF])
        pt = ps("pt", [P, 2, BLK * P])
        pm = ps("pm", [P, 512])
        pc = ps("pc", [P, 512])

        def sems(names):
            return [sem(n) for n in names.split()]

        w0_in, small_in, ffn_in = sems("w0_in small_in ffn_in")
        ident_zeroed, ident_made, ones_made, node_made, bq_scaled = sems("ident_zeroed ident_made ones_made node_made bq_scaled")
        x_in = [sem(f"x_in{g}") for g in range(NT // GT)]
        (A_step, A_normed, A_transposed, A_reluT, A_projected, A_copied, A_scored, A_rowed, A_rowcopied) = sems(
            "A_step A_normed A_transposed A_reluT A_projected A_copied A_scored A_rowed A_rowcopied")
        (adjB_in, B_masked, B_scored, B_leaky, B_max, B_neg, B_probs, B_T, B_evac, B_av, B_expneg, B_step, B_pool, B_hsT, B_hsTcopied,
         B_projK, B_projV, B_whole, B_vcopied, key_split_out, key_stacked) = sems(
            "adjB_in B_masked B_scored B_leaky B_max B_neg B_probs B_T B_evac B_av B_expneg B_step B_pool B_hsT B_hsTcopied "
            "B_projK B_projV B_whole B_vcopied key_split_out key_stacked")
        (Q_step, Q_pool, Q_T, Q_Tcopied, Q_proj, Q_whole, query_split_out, targets_out) = sems(
            "Q_step Q_pool Q_T Q_Tcopied Q_proj Q_whole query_split_out targets_out")
        target_in_sem = [sem(f"target_in{i}") for i in range(2)]
        query_stacked = [sem(f"query_stacked{i}") for i in range(2)]
        (adjC_in, C_masked, C_qk, C_max, C_neg, C_probs, C_T, C_evac_act, C_evac_dve, C_av, C_recip, C_ctx, C_biased) = sems(
            "adjC_in C_masked C_qk C_max C_neg C_probs C_T C_evac_act C_evac_dve C_av C_recip C_ctx C_biased")
        (D_rows, D_ctxT, D_ctxTcopied, D_attn, D_step, D_pool, D_postT, D_postTcopied, D_hidden, D_gelu, D_ff, D_out,
         targets_back, stored) = sems(
            "D_rows D_ctxT D_ctxTcopied D_attn D_step D_pool D_postT D_postTcopied D_hidden D_gelu D_ff D_out "
            "targets_back stored")
        A_roots, B_roots, Q_roots, D_roots = sems("A_roots B_roots Q_roots D_roots")
        B_STEPS, B_POOLS, Q_STEPS, Q_POOLS, D_STEPS, D_POOLS = 14, 5, 4, 5, 6, 4
        SMALL = 13 * 16

        def rows(dram, t):
            return dram[bass.ds(t * P, P), :]

        def cols(t):
            return bass.ds(t * P, P)

        def split_rows(dram, part, t):
            return dram[part, :, cols(t)].rearrange("(c p) n -> p c n", p=P)

        def stack_rows(dram, part, t):
            return dram[part, :, cols(t)].rearrange("(h d) n -> d h n", d=HD)

        def after(eng, s, value):
            if not isinstance(value, int) or value > 0:
                eng.wait_ge(s, value)

        def layer_norm(eng, chain, dst, src, roots, root):
            chain.link(eng.bn_stats(stats[:], src), apart)
            chain.link(eng.bn_aggr(mv[:], stats[:]))
            chain.link(eng.tensor_scalar(mv[:, 1:2], mv[:, 1:2], EPS, None, ALU.add))
            eng.wait_ge(roots, root)
            return eng.tensor_scalar(dst, src, mv[:, 0:1], rstd[:], ALU.subtract, ALU.mult)

        def inverse_root(pool, steps, step, roots):
            pool.wait_ge(steps, step)
            pool.tensor_tensor(rstd[:], mv[:, 1:2], minus_half[:], ALU.pow).then_inc(roots, 1)

        def apart(eng, *waits):
            waits = [(s, v if isinstance(v, int) else eng.compute_val(v)) for s, v in waits if not isinstance(v, int) or v > 0]
            if waits:
                eng.wait_ge(ident_made, 1)
            for s, value in waits:
                eng.wait_ge(s, value)

        def unit(v, h):
            u = v.ahead(h // HEADS)
            return u, h % HEADS, u.t * HEADS + h % HEADS

        def group_loop(eng, step):
            step(-1)
            step(0)
            with eng.Fori(1, NG - 1) as g:
                step(g)
            step(NG - 1)

        DVE_CHUNKS, ACT_CHUNKS = (0, 2), (1, 3)

        def evacuated(eng, n, c):
            on, s = (DVE_CHUNKS, C_evac_dve) if c in DVE_CHUNKS else (ACT_CHUNKS, C_evac_act)
            after(eng, s, n * len(on) + on.index(c) + 1)

        block = ctx.enter_context(nc.Block())

        @block.sync
        def _(sp):
            xv = x.rearrange("(g t p) d -> g p t d", p=P, t=GT)
            sp.dma_start(xres[:, 0:GT, :], xv[0]).then_inc(x_in[0], 16)
            sp.dma_start(w0, W0.rearrange("(c p) n -> p c n", p=P)).then_inc(w0_in, 16)
            for i in range(2):
                sp.dma_start(att[:, i, :], attn0[i * D:(i + 1) * D, :].rearrange("d o -> o d").broadcast_to([P, D])).then_inc(w0_in, 16)
            for g in range(1, NT // GT):
                sp.dma_start(xres[:, GT * g:GT * g + GT, :], xv[g]).then_inc(x_in[g], 16)
            for dst, w in ((wq, Wq), (wk, Wk), (wv, Wv), (wo, Wo)):
                sp.dma_start(dst[:], w.rearrange("(c p) n -> p c n", p=P)).then_inc(small_in, 16)
            for dst, v in ((ln1s, ln1_scale), (ln1b, ln1_bias), (ln2s, ln2_scale), (ln2b, ln2_bias), (bvr, bv), (bor, bo)):
                sp.dma_start(dst[:], v.rearrange("(a d) -> a d", a=1).broadcast_to([P, D])).then_inc(small_in, 16)
            with nc.allow_non_contiguous_dma(reason="a few thousand single values, once"):
                for dst, v in ((bqc, bq), (bkc, bk), (node_i, nodemask)):
                    sp.dma_start(dst[:], v.rearrange("(c p) -> p c", p=P)).then_inc(small_in, 16)

            def gat_step(v):
                u = v.ahead(2)
                if u.real():
                    apart(sp, (B_masked, u.t))
                    sp.dma_start(adj_in, rows(adj, u.t)).then_inc(adjB_in, 16)
                if v.real():
                    apart(sp, (B_pool, v.t * B_POOLS + B_POOLS))
                    sp.dma_start(split_rows(key_dram, 0, v.t), part_a[:].bitcast(F32)).then_inc(key_split_out, 16)
                    sp.dma_start(split_rows(key_dram, 1, v.t), part_b[:].bitcast(F32)).then_inc(key_split_out, 16)
                    apart(sp, (key_split_out, v.t * 32 + 32))
                    for r, part in enumerate((0, 1, 0, 1)):
                        sp.dma_start(key_stack[r * HD:(r + 1) * HD, :, cols(v.t)].bitcast(F32), stack_rows(key_dram, part, v.t)).then_inc(key_stacked, 16)
            tile_loop(sp, gat_step, 2)

            def mha_step(v):
                u = v.ahead(2)
                if u.real():
                    apart(sp, (Q_step, (u.t - 1) * Q_STEPS))
                    sp.dma_start(target_in[:, u.parity, :], rows(h_target, u.t)).then_inc(target_in_sem[u.parity], 16)
                u = v.ahead(1)
                if u.real():
                    apart(sp, (C_masked, u.t))
                    if u.static and u.t == 0:
                        sp.wait_ge(B_masked, NT)
                    sp.dma_start(adj_in, rows(adj, u.t)).then_inc(adjC_in, 16)
                    apart(sp, (Q_pool, u.t * Q_POOLS + 3))
                    sp.dma_start(rows(target_dram, u.t), normed[:, 0, :]).then_inc(targets_out, 16)
                    apart(sp, (Q_pool, u.t * Q_POOLS + Q_POOLS))
                    sp.dma_start(split_rows(query_dram, 0, u.t), part_a[:].bitcast(F32)).then_inc(query_split_out, 16)
                    sp.dma_start(split_rows(query_dram, 1, u.t), part_b[:].bitcast(F32)).then_inc(query_split_out, 16)
                    apart(sp, (query_split_out, u.t * 32 + 32))
                    apart(sp, (C_qk, (u.t - 1) * HEADS * 2))
                    for r, part in enumerate((0, 0, 1, 1)):
                        sp.dma_start(query_stack[r * HD:(r + 1) * HD, u.parity, :, :].bitcast(F32), stack_rows(query_dram, part, u.t)).then_inc(query_stacked[u.parity], 16)
            tile_loop(sp, mha_step, 2)

            sp.wait_ge(C_T, UNITS * CH)
            sp.dma_start(w1, W1.rearrange("(c p) n -> p c n", p=P)).then_inc(ffn_in, 16)
            sp.dma_start(w2, W2.rearrange("(c p) n -> p c n", p=P)).then_inc(ffn_in, 16)
            sp.wait_ge(C_masked, NT)
            sp.wait_ge(targets_out, NT * 16)
            grouped = "(t p) d -> p t d"

            def ffn_step(v):
                if not isinstance(v, int) or v + 1 < NG:
                    apart(sp, (D_step, (v + 1) * GT * D_STEPS))
                    sp.dma_start(target_rows, target_dram[bass.ds((v + 1) * GT * P, GT * P), :].rearrange(grouped, p=P)).then_inc(targets_back, 16)
                if not isinstance(v, int) or v >= 0:
                    apart(sp, (D_out, (v + 1) * GT))
                    sp.dma_start(out[bass.ds(v * GT * P, GT * P), :].rearrange(grouped, p=P), xres[:, bass.ds(v * GT, GT), :]).then_inc(stored, 16)
            group_loop(sp, ffn_step)
            sp.wait_ge(stored, NG * 16)

        @block.gpsimd
        def _(pool):
            pool.memset(ident[:], 0.0).then_inc(ident_zeroed, 1)
            pool.wait_ge(ident_zeroed, 1)
            pool.affine_select(out=ident[:], in_=ident[:], compare_op=ALU.not_equal, fill=1.0, base=0,
                               pattern=[[-1, P]], channel_multiplier=1).then_inc(ident_made, 1)
            pool.memset(minus_half[:], -0.5).then_inc(ones_made, 1)
            pool.memset(hproj[:, :, D:D + 1], 1.0).then_inc(ones_made, 1)
            pool.memset(value[:, :, :, HD:HD + 1], 1.0).then_inc(ones_made, 1)
            pool.wait_ge(small_in, SMALL)
            pool.tensor_scalar(node[:], node_i[:], 1, None, ALU.is_equal).then_inc(node_made, 1)
            pool.tensor_scalar(bqc[:], bqc[:], QSCALE, None, ALU.mult).then_inc(bq_scaled, 1)
            pool.wait_ge(node_made, 1)
            pool.wait_ge(ones_made, 3)

            def gat_step(v):
                u = v.ahead(2)
                if u.real():
                    apart(pool, (adjB_in, (u.t + 1) * 16), (B_max, u.t - 1))
                    pool.tensor_scalar(mask[:, u.parity, :], adj_in, 0, MASKED, ALU.is_le, ALU.mult).then_inc(B_masked, 1)
                if v.real():
                    chain = Chain(pool, B_pool, v.t * B_POOLS)
                    inverse_root(pool, B_step, v.t * B_STEPS + 8, B_roots)
                    inverse_root(pool, B_step, v.t * B_STEPS + 13, B_roots)
                    pool.wait_ge(B_step, (v.t + 1) * B_STEPS)
                    chain.link(pool.tensor_tensor(affine[:], row3[:], ln1s[:], ALU.mult))
                    chain.link(pool.tensor_tensor(affine[:], affine[:], ln1b[:], ALU.add))
                    pool.wait_ge(B_hsT, v.t)
                    chain.link(pool.tensor_tensor(normed[:, 0, :], affine[:], node[:, bass.ds(v.t, 1)].broadcast_to([P, D]), ALU.mult))
                    apart(pool, (B_whole, (v.t + 1) * KC), (key_split_out, v.t * 32))
                    chain.link(pool.tensor_copy(part_a[:], whole[:]))
                    chain.link(pool.tensor_tensor(part_b[:], whole[:], part_a[:].bitcast(F32), ALU.subtract))
            def root_step(v):
                if v.ahead(2).real():
                    inverse_root(pool, A_step, (v.ahead(2).t + 1) * 3, A_roots)
            tile_loop(pool, root_step, 2)

            pool.wait_ge(A_transposed, NT)
            tile_loop(pool, gat_step, 2)

            def mha_step(v):
                u = v.ahead(1)
                if u.real():
                    apart(pool, (adjC_in, (u.t + 1) * 16), (C_max, (u.t - 1) * HEADS * 2))
                    pool.tensor_scalar(mask[:, u.parity, :], adj_in, 0, MASKED, ALU.is_equal, ALU.mult).then_inc(C_masked, 1)
                    chain = Chain(pool, Q_pool, u.t * Q_POOLS)
                    inverse_root(pool, Q_step, u.t * Q_STEPS + 3, Q_roots)
                    pool.wait_ge(Q_step, (u.t + 1) * Q_STEPS)
                    chain.link(pool.tensor_tensor(affine[:], row3[:], ln1s[:], ALU.mult))
                    chain.link(pool.tensor_tensor(affine[:], affine[:], ln1b[:], ALU.add))
                    after(pool, Q_T, u.t)
                    after(pool, targets_out, u.t * 16)
                    chain.link(pool.tensor_tensor(normed[:, 0, :], affine[:], node[:, bass.ds(u.t, 1)].broadcast_to([P, D]), ALU.mult))
                    apart(pool, (Q_whole, (u.t + 1) * KC), (query_split_out, u.t * 32))
                    chain.link(pool.tensor_copy(part_a[:], whole[:]))
                    chain.link(pool.tensor_tensor(part_b[:], whole[:], part_a[:].bitcast(F32), ALU.subtract))
                if v.real():
                    pool.wait_ge(C_ctx, v.t + 1)
                    here = context[:, bass.ds(v.t, 1), :].rearrange("p t d -> p (t d)")
                    pool.tensor_tensor(here, here, bvr[:], ALU.add).then_inc(C_biased, 1)
            pool.wait_ge(B_max, NT)
            pool.wait_ge(B_hsT, NT)
            pool.wait_ge(key_split_out, NT * 32)
            tile_loop(pool, mha_step, 1)

            def ffn_step(v):
                if isinstance(v, int) and v + 1 >= NG:
                    return
                for k in range(GT):
                    t = (v + 1) * GT + k
                    after(pool, D_ctxT, t - (GT - 1))
                    pool.tensor_copy(ctx_rows[:, k, :], context[:, bass.ds(t, 1), :].rearrange("p t d -> p (t d)")).then_inc(D_rows, 1)
                for k in range(GT):
                    t = (v + 1) * GT + k
                    chain = Chain(pool, D_pool, t * D_POOLS)
                    inverse_root(pool, D_step, t * D_STEPS + 5, D_roots)
                    pool.wait_ge(D_step, (t + 1) * D_STEPS)
                    chain.link(pool.tensor_tensor(affine[:], row3[:], ln2s[:], ALU.mult))
                    chain.link(pool.tensor_tensor(affine[:], affine[:], ln2b[:], ALU.add))
                    after(pool, D_postT, t - (GT - 1))
                    chain.link(pool.tensor_tensor(post[:, k, :], affine[:], node[:, bass.ds(t, 1)].broadcast_to([P, D]), ALU.mult))
                    here = xres[:, bass.ds(t, 1), :].rearrange("p t d -> p (t d)")
                    chain.link(pool.tensor_tensor(here, here, post[:, k, :], ALU.add))
            pool.wait_ge(C_biased, NT)
            pool.wait_ge(C_av, UNITS * CH)
            group_loop(pool, ffn_step)

        @block.tensor
        def _(pe):
            def transposes(dst, src, ready):
                for k in range(KC):
                    last = pe.transpose(dst[:, k * P:(k + 1) * P], src[:, k * P:(k + 1) * P], ident[:])
                last.then_inc(ready, 1)

            def project(dst, lhsT, w, ready):
                for c in range(KC):
                    last = pe.matmul(dst, lhsT[:, c, :], w[:, c, :], start=(c == 0), stop=(c == KC - 1))
                last.then_inc(ready, 1)

            def project_heads(dst, w, rhsT, ready):
                for m in range(KC):
                    for c in range(KC):
                        last = pe.matmul(dst[:, m * P:(m + 1) * P], w[:, c, m * P:(m + 1) * P], rhsT[:, c, :],
                                         start=(c == 0), stop=(c == KC - 1))
                last.then_inc(ready, 1)

            def proj_step(v):
                u = v.ahead(2)
                if u.real():
                    pe.wait_ge(A_normed, u.t + 1)
                    after(pe, A_reluT, u.t - 1)
                    transposes(pt[:, u.parity, :], normed[:, u.parity, :], A_transposed)
                u = v.ahead(1)
                if u.real():
                    pe.wait_ge(A_reluT, u.t + 1)
                    after(pe, A_copied, u.t - 1)
                    project(pq[:, u.parity, 0:D], normedT[:, u.parity], w0, A_projected)
                if v.real():
                    pe.wait_ge(A_scored, (v.t + 1) * 2)
                    after(pe, A_rowcopied, v.t)
                    pe.matmul(pm[:, 0:P], s2[:, v.parity:v.parity + 1].broadcast_to([P, P]), ident[:],
                              start=True, stop=True).then_inc(A_rowed, 1)
            pe.wait_ge(ident_made, 1)
            pe.wait_ge(w0_in, 48)
            tile_loop(pe, proj_step, 2)

            def gat_step(v):
                u = v.ahead(1)
                if u.real():
                    def weigh(c):
                        pe.wait_ge(B_evac, u.t * CH + c + 1)
                        if c == 0:
                            after(pe, B_step, (u.t - 1) * B_STEPS + 2)
                        for k in range(BLK):
                            last = pe.matmul(pc[:, 0:D + 1], probsT[:, c, k * P:(k + 1) * P], hproj[:, c * BLK + k, :],
                                             start=(c + k == 0), stop=(c == CH - 1 and k == BLK - 1))
                        last.then_inc(B_av, 1)

                    pe.wait_ge(B_probs, u.t + 1)
                    for c in range(CH):
                        after(pe, B_evac, u.t * CH + c - 1)
                        for k in range(BLK):
                            last = pe.transpose(pt[:, c % 2, k * P:(k + 1) * P],
                                                ring[:, u.parity, (c * BLK + k) * P:(c * BLK + k + 1) * P], ident[:])
                        last.then_inc(B_T, 1)
                        if c:
                            weigh(c - 1)
                    weigh(CH - 1)
                if v.real():
                    pe.wait_ge(B_pool, v.t * B_POOLS + 3)
                    after(pe, B_hsTcopied, v.t)
                    transposes(pm, normed[:, 0, :], B_hsT)
                    pe.wait_ge(B_hsTcopied, v.t + 1)
                    after(pe, B_whole, v.t * KC)
                    project_heads(pq[:, 0, :], wk, normedT[:, 0], B_projK)
                    after(pe, B_vcopied, v.t)
                    project(pq[:, 1, 0:D], normedT[:, 0], wv, B_projV)
            pe.wait_ge(A_reluT, NT)
            pe.wait_ge(A_copied, NT)
            pe.wait_ge(A_rowcopied, NT)
            pe.wait_ge(ones_made, 3)
            pe.wait_ge(small_in, SMALL)
            tile_loop(pe, gat_step, 2)

            def mha_step(v):
                for h in range(HEADS):
                    uq, hq, nq = unit(v, h + 3)
                    ut, ht, n_t = unit(v, h + 1)
                    for c in range(CH):
                        if uq.real() and c % 2 == 0:
                            half = c // 2
                            if hq == 0 and half == 0:
                                pe.wait_ge(query_stacked[uq.parity], (uq.pair + 1) * 64)
                            after(pe, C_max, nq * 2 + half - 1)
                            for k in range(2):
                                at = half * HALF + k * 512
                                last = pe.matmul(pq[:, half, k * 512:(k + 1) * 512], query_stack[:, uq.parity, hq, :],
                                                 key_stack[:, hq, at:at + 512], start=True, stop=True)
                            last.then_inc(C_qk, 1)
                        if ut.real():
                            if c == 0:
                                pe.wait_ge(C_probs, n_t + 1)
                            if c >= 2:
                                evacuated(pe, n_t, c - 2)
                            elif not (ut.static and n_t == 0):
                                evacuated(pe, n_t - 1, c + 2)
                            for k in range(BLK):
                                last = pe.transpose(pt[:, c % 2, k * P:(k + 1) * P],
                                                    ring[:, ht % 4, (c * BLK + k) * P:(c * BLK + k + 1) * P], ident[:])
                            last.then_inc(C_T, 1)
                        if v.real():
                            evacuated(pe, v.t * HEADS + h, c)
                            if h == 0 and c == 0:
                                after(pe, C_ctx, v.t)
                            for k in range(BLK):
                                last = pe.matmul(pc[:, h * (HD + 1):(h + 1) * (HD + 1)], probsT[:, c, k * P:(k + 1) * P],
                                                 value[:, c * BLK + k, h, :], start=(c + k == 0),
                                                 stop=(c == CH - 1 and k == BLK - 1))
                            last.then_inc(C_av, 1)
                    u = v.ahead(1)
                    if u.real() and h == 1:
                        pe.wait_ge(Q_pool, u.t * Q_POOLS + 3)
                        after(pe, Q_whole, u.t * KC)
                        transposes(pm, normed[:, 0, :], Q_T)
                    if u.real() and h == 2:
                        pe.wait_ge(Q_Tcopied, u.t + 1)
                        project_heads(pm, wq, normedT[:, 0], Q_proj)
            pe.wait_ge(B_hsTcopied, NT)
            pe.wait_ge(B_whole, NT * KC)
            pe.wait_ge(B_vcopied, NT)
            pe.wait_ge(B_evac, NT * CH)
            pe.wait_ge(B_step, (NT - 1) * B_STEPS + 2)
            pe.wait_ge(key_stacked, NT * 64)
            tile_loop(pe, mha_step, 1)

            def ffn_step(v):
                ahead = not isinstance(v, int) or v + 1 < NG
                now = not isinstance(v, int) or v >= 0
                if ahead:
                    for k in range(GT + 1):
                        t = (v + 1) * GT + k
                        if k < GT:
                            pe.wait_ge(D_rows, t + 1)
                            after(pe, D_ctxTcopied, t - 1)
                            after(pe, D_postTcopied, (v + 1) * GT)
                            transposes(pt[:, k % 2, :], ctx_rows[:, k, :], D_ctxT)
                        if k:
                            t = t - 1
                            pe.wait_ge(D_ctxTcopied, t + 1)
                            after(pe, D_step, (t - 2) * D_STEPS + 1)
                            project((pm, pc)[(k - 1) % 2][:, 0:D], normedT[:, (k - 1) % 2], wo, D_attn)
                if now:
                    pe.wait_ge(D_postTcopied, (v + 1) * GT)
                    for m in range(MC):
                        n = v * MC + m
                        if not (isinstance(n, int) and n < 2):
                            if m < 2:
                                after(pe, D_gelu, v * MC)
                            else:
                                after(pe, D_gelu, n - 1)
                        for c in range(KC):
                            last = pe.matmul(pq[:, 0, (m % 2) * 512:(m % 2 + 1) * 512], w1[:, c, m * P:(m + 1) * P], postT[:, c, :],
                                             start=(c == 0), stop=(c == KC - 1))
                        last.then_inc(D_hidden, 1)
                for k in range(GT):
                    if ahead:
                        t = (v + 1) * GT + k
                        pe.wait_ge(D_pool, t * D_POOLS + 3)
                        after(pe, D_ctxTcopied, (v + 2) * GT)
                        if k >= 2:
                            after(pe, D_postTcopied, t - 1)
                        transposes(pt[:, k % 2, :], post[:, k, :], D_postT)
                    if now:
                        t = v * GT + k
                        if k == 0:
                            pe.wait_ge(D_gelu, (v + 1) * MC)
                        if k < 2:
                            after(pe, D_out, v * GT)
                        else:
                            after(pe, D_out, t - 1)
                        for m in range(MC):
                            last = pe.matmul(pq[:, 1, (k % 2) * 512:(k % 2) * 512 + D], hiddenT[:, m, k * P:(k + 1) * P], w2[:, m, :],
                                             start=(m == 0), stop=(m == MC - 1))
                        last.then_inc(D_ff, 1)
            pe.wait_ge(Q_whole, NT * KC)
            pe.wait_ge(C_ctx, NT)
            pe.wait_ge(C_max, UNITS * 2)
            evacuated(pe, UNITS - 1, CH - 1)
            evacuated(pe, UNITS - 1, CH - 2)
            pe.wait_ge(ffn_in, 32)
            group_loop(pe, ffn_step)

        @block.scalar
        def _(act):
            def proj_step(v):
                u = v.ahead(2)
                if u.real():
                    act.wait_ge(A_transposed, u.t + 1)
                    after(act, A_projected, u.t - 1)
                    act.activation(normedT[:, u.parity].rearrange("p c n -> p (c n)"), pt[:, u.parity, 0:D], ACT.Relu).then_inc(A_reluT, 1)
                u = v.ahead(1)
                if u.real():
                    act.wait_ge(A_projected, u.t + 1)
                    act.copy(hproj[:, bass.ds(u.t, 1), 0:D].rearrange("p t d -> p (t d)"), pq[:, u.parity, 0:D]).then_inc(A_copied, 1)
                if v.real():
                    act.wait_ge(A_rowed, v.t + 1)
                    act.copy(src_row[:, cols(v.t)], pm[:, 0:P]).then_inc(A_rowcopied, 1)
            tile_loop(act, proj_step, 2)

            def gat_step(v):
                u = v.ahead(1)

                def evacuate(c):
                    act.wait_ge(B_T, u.t * CH + c + 1)
                    after(act, B_av, u.t * CH + c - 3)
                    act.copy(probsT[:, c, :], pt[:, c % 2, :]).then_inc(B_evac, 1)

                if u.real():
                    evacuate(0)
                    evacuate(1)
                w = v.ahead(2)
                if w.real():
                    after(act, B_T, (w.t - 1) * CH)
                    act.activation(ring[:, w.parity, :], src_row, ACT.Identity, bias=s1[:, bass.ds(w.t, 1)],
                                   scale=1.0).then_inc(B_scored, 1)
                if v.real():
                    act.wait_ge(B_step, v.t * B_STEPS + 3)
                    act.activation(row2[:], row2[:], ACT.Exp).then_inc(B_expneg, 1)
                if u.real():
                    evacuate(2)
                    evacuate(3)
                if w.real():
                    act.wait_ge(B_neg, w.t + 1)
                    act.activation(ring[:, w.parity, :], ring[:, w.parity, :], ACT.Exp, bias=negmax[:, w.parity:w.parity + 1],
                                   scale=1.0).then_inc(B_probs, 1)
                if v.real():
                    act.wait_ge(B_hsT, v.t + 1)
                    after(act, B_projV, v.t)
                    act.copy(normedT[:, 0].rearrange("p c n -> p (c n)"), pm[:, 0:D]).then_inc(B_hsTcopied, 1)
                    act.wait_ge(B_projK, v.t + 1)
                    after(act, B_pool, v.t * B_POOLS)
                    for c in range(KC):
                        act.activation(whole[:, c, :], pq[:, 0, c * P:(c + 1) * P], ACT.Identity, bias=bkc[:, c:c + 1], scale=1.0).then_inc(B_whole, 1)
                    act.wait_ge(B_projV, v.t + 1)
                    act.copy(value[:, bass.ds(v.t, 1), :, 0:HD].rearrange("p t h d -> p (t h) d"),
                             pq[:, 1, 0:D].rearrange("p (h d) -> p h d", d=HD)).then_inc(B_vcopied, 1)
            act.wait_ge(A_rowcopied, NT)
            act.wait_ge(A_scored, NT * 2)
            act.wait_ge(A_projected, NT)
            act.wait_ge(small_in, SMALL)
            tile_loop(act, gat_step, 2)

            def mha_step(v):
                for h in range(HEADS):
                    ut, ht, n_t = unit(v, h + 1)
                    ue, he, n_e = unit(v, h + 2)

                    def evacuate(c):
                        act.wait_ge(C_T, n_t * CH + c + 1)
                        after(act, C_av, n_t * CH + c - 3)
                        act.copy(probsT[:, c, :], pt[:, c % 2, :]).then_inc(C_evac_act, 1)

                    if ut.real():
                        evacuate(ACT_CHUNKS[0])
                    if ue.real():
                        act.wait_ge(C_neg, n_e + 1)
                        act.activation(ring[:, he % 4, :], ring[:, he % 4, :], ACT.Exp, bias=negmax[:, he % 4:he % 4 + 1],
                                       scale=1.0).then_inc(C_probs, 1)
                    if ut.real():
                        for c in ACT_CHUNKS[1:]:
                            evacuate(c)
                    u = v.ahead(1)
                    if u.real() and h == 1:
                        act.wait_ge(Q_T, u.t + 1)
                        after(act, Q_proj, u.t)
                        act.copy(normedT[:, 0].rearrange("p c n -> p (c n)"), pm[:, 0:D]).then_inc(Q_Tcopied, 1)
                    if u.real() and h == 2:
                        act.wait_ge(Q_proj, u.t + 1)
                        after(act, Q_pool, u.t * Q_POOLS)
                        for c in range(KC):
                            act.activation(whole[:, c, :], pm[:, c * P:(c + 1) * P], ACT.Identity, bias=bqc[:, c:c + 1],
                                           scale=QSCALE).then_inc(Q_whole, 1)
            act.wait_ge(B_pool, NT * B_POOLS)
            act.wait_ge(B_av, NT * CH)
            act.wait_ge(bq_scaled, 1)
            tile_loop(act, mha_step, 1)

            def ffn_step(v):
                ahead = not isinstance(v, int) or v + 1 < NG
                now = not isinstance(v, int) or v >= 0
                if ahead:
                    for k in range(GT):
                        t = (v + 1) * GT + k
                        act.wait_ge(D_ctxT, t + 1)
                        after(act, D_attn, t - 1)
                        act.copy(normedT[:, k % 2].rearrange("p c n -> p (c n)"), pt[:, k % 2, 0:D]).then_inc(D_ctxTcopied, 1)
                if now:
                    after(act, D_ff, v * GT)
                    for m in range(MC):
                        act.wait_ge(D_hidden, v * MC + m + 1)
                        act.activation(hiddenT[:, m, :], pq[:, 0, (m % 2) * 512:(m % 2 + 1) * 512], ACT.Gelu_apprx_tanh).then_inc(D_gelu, 1)
                if ahead:
                    for k in range(GT):
                        t = (v + 1) * GT + k
                        act.wait_ge(D_postT, t + 1)
                        after(act, D_hidden, (v + 1) * MC)
                        act.copy(postT[:, :, k * P:(k + 1) * P], pt[:, k % 2, 0:D].rearrange("p (c n) -> p c n", n=P)).then_inc(D_postTcopied, 1)
            act.wait_ge(C_T, UNITS * CH)
            act.wait_ge(C_av, UNITS * CH)
            group_loop(act, ffn_step)

        @block.vector
        def _(dve):
            def proj_step(v):
                u = v.ahead(2)
                if u.real():
                    chain = Chain(dve, A_step, u.t * 3)
                    src = xres[:, bass.ds(u.t, 1), :].rearrange("p t d -> p (t d)")
                    if u.static:
                        dve.wait_ge(x_in[u.t // GT], 16)
                    apart(dve, (A_transposed, u.t - 1))
                    layer_norm(dve, chain, normed[:, u.parity, :], src, A_roots, u.t + 1).then_inc(A_normed, 1)
                u = v.ahead(1)
                if u.real():
                    dve.wait_ge(A_copied, u.t + 1)
                    after(dve, A_rowed, u.t - 1)
                    after(dve, A_scored, u.t * 2)
                    here = hproj[:, bass.ds(u.t, 1), 0:D].rearrange("p t d -> p (t d)")
                    dve.scalar_tensor_tensor(out=row1[:], in0=here, scalar=1.0, in1=att[:, 0, :], op0=ALU.mult, op1=ALU.mult,
                                             accum_out=s1[:, bass.ds(u.t, 1)]).then_inc(A_scored, 1)
                    dve.scalar_tensor_tensor(out=row2[:], in0=here, scalar=1.0, in1=att[:, 1, :], op0=ALU.mult, op1=ALU.mult,
                                             accum_out=s2[:, u.parity:u.parity + 1]).then_inc(A_scored, 1)
            dve.wait_ge(w0_in, 48)
            for g in range(NT // GT):
                dve.wait_ge(x_in[g], 16)
            tile_loop(dve, proj_step, 2)

            def gat_step(v):
                if v.real():
                    chain = Chain(dve, B_step, v.t * B_STEPS)
                    dve.wait_ge(B_av, (v.t + 1) * CH)
                    chain.link(dve.reciprocal(recip[:, 0:1], pc[:, D:D + 1]))
                    chain.link(dve.tensor_scalar(row1[:], pc[:, 0:D], recip[:, 0:1], None, ALU.mult))
                    chain.link(dve.tensor_scalar(row2[:], row1[:], 0.0, None, ALU.min))
                w = v.ahead(2)
                if w.real():
                    s = ring[:, w.parity, :]
                    dve.wait_ge(B_scored, w.t + 1)
                    dve.scalar_tensor_tensor(out=s, in0=s, scalar=ALPHA, in1=s, op0=ALU.mult, op1=ALU.max).then_inc(B_leaky, 1)
                    apart(dve, (B_leaky, w.t + 1), (B_masked, w.t + 1))
                    dve.tensor_tensor_reduce(s, s, mask[:, w.parity, :], 1.0, LOWEST, ALU.add, ALU.max,
                                             rowmax[:, w.parity, 0:1]).then_inc(B_max, 1)
                    dve.wait_ge(B_max, w.t + 1)
                    dve.tensor_scalar(negmax[:, w.parity:w.parity + 1], rowmax[:, w.parity, 0:1], -1.0, None, ALU.mult).then_inc(B_neg, 1)
                if v.real():
                    here = xres[:, bass.ds(v.t, 1), :].rearrange("p t d -> p (t d)")
                    dve.wait_ge(B_expneg, v.t + 1)
                    chain.link(dve.scalar_tensor_tensor(out=row1[:], in0=row2[:], scalar=-1.0, in1=row1[:], op0=ALU.add, op1=ALU.max))
                    chain.link(dve.tensor_tensor(here, here, row1[:], ALU.add), apart)
                    chain.link(layer_norm(dve, chain, row1[:], here, B_roots, v.t * 2 + 1))
                    after(dve, B_pool, v.t * B_POOLS)
                    chain.link(dve.tensor_scalar(row1[:], row1[:], 0.0, None, ALU.max), apart)
                    chain.link(layer_norm(dve, chain, row3[:], row1[:], B_roots, v.t * 2 + 2))
                    assert chain.n == B_STEPS
            dve.wait_ge(A_scored, NT * 2)
            tile_loop(dve, gat_step, 2)

            def mha_step(v):
                for h in range(HEADS):
                    um, hm, n_m = unit(v, h + 3)
                    ut, ht, n_t = unit(v, h + 1)

                    def evacuate(c):
                        dve.wait_ge(C_T, n_t * CH + c + 1)
                        after(dve, C_av, n_t * CH + c - 3)
                        dve.tensor_copy(probsT[:, c, :], pt[:, c % 2, :]).then_inc(C_evac_dve, 1)

                    def mask_and_max(half):
                        if hm == 0 and half == 0:
                            dve.wait_ge(C_masked, um.t + 1)
                        if half == 0:
                            after(dve, C_T, (n_m - 3) * CH)
                        apart(dve, (C_qk, n_m * 2 + half + 1))
                        at = slice(half * HALF, (half + 1) * HALF)
                        dve.tensor_tensor_reduce(ring[:, hm % 4, at], pq[:, half, :], mask[:, um.parity, at], 1.0, LOWEST,
                                                 ALU.add, ALU.max, rowmax[:, hm % 4, half:half + 1]).then_inc(C_max, 1)

                    if ut.real():
                        evacuate(DVE_CHUNKS[0])
                    if um.real():
                        mask_and_max(0)
                    if ut.real():
                        for c in DVE_CHUNKS[1:]:
                            evacuate(c)
                    if um.real():
                        mask_and_max(1)
                        dve.wait_ge(C_max, n_m * 2 + 2)
                        dve.tensor_reduce(negmax[:, hm % 4:hm % 4 + 1], rowmax[:, hm % 4, :], mybir.AxisListType.X, ALU.max,
                                          negate=True).then_inc(C_neg, 1)
                    u = v.ahead(1)
                    if u.real() and h == 0:
                        chain = Chain(dve, Q_step, u.t * Q_STEPS)
                        apart(dve, (target_in_sem[u.parity], (u.pair + 1) * 16), (Q_pool, u.t * Q_POOLS))
                        chain.link(layer_norm(dve, chain, row3[:], target_in[:, u.parity, :], Q_roots, u.t + 1))
                        assert chain.n == Q_STEPS
                if v.real():
                    sums = pc[:, 0:HEADS * (HD + 1)].rearrange("p (h d) -> p h d", d=HD + 1)
                    dve.wait_ge(C_av, (v.t + 1) * HEADS * CH)
                    dve.reciprocal(recip[:, :].rearrange("p (h o) -> p h o", o=1), sums[:, :, HD:HD + 1]).then_inc(C_recip, 1)
                    dve.wait_ge(C_recip, v.t + 1)
                    dve.tensor_tensor(context[:, bass.ds(v.t, 1), :].rearrange("p t (h d) -> p (t h) d", d=HD), sums[:, :, 0:HD],
                                      recip[:, :].rearrange("p (h o) -> p h o", o=1).broadcast_to([P, HEADS, HD]), ALU.mult).then_inc(C_ctx, 1)
            dve.wait_ge(B_T, NT * CH)
            dve.wait_ge(B_av, NT * CH)
            dve.wait_ge(B_scored, NT)
            dve.wait_ge(B_pool, NT * B_POOLS)
            tile_loop(dve, mha_step, 1)

            def ffn_step(v):
                ahead = not isinstance(v, int) or v + 1 < NG
                now = not isinstance(v, int) or v >= 0
                if ahead:
                    dve.wait_ge(targets_back, (v + 2) * 16)
                    for k in range(GT):
                        t = (v + 1) * GT + k
                        chain = Chain(dve, D_step, t * D_STEPS)
                        dve.wait_ge(D_attn, t + 1)
                        after(dve, D_pool, t * D_POOLS)
                        chain.link(dve.tensor_tensor(row1[:], (pm, pc)[k % 2][:, 0:D], bor[:], ALU.add))
                        chain.link(dve.scalar_tensor_tensor(out=row1[:], in0=row1[:], scalar=node[:, bass.ds(t, 1)], in1=target_rows[:, k, :],
                                                            op0=ALU.mult, op1=ALU.add), apart)
                        chain.link(layer_norm(dve, chain, row3[:], row1[:], D_roots, t + 1))
                        assert chain.n == D_STEPS
                if now:
                    for k in range(GT):
                        t = v * GT + k
                        here = xres[:, bass.ds(t, 1), :].rearrange("p t d -> p (t d)")
                        dve.wait_ge(D_ff, t + 1)
                        dve.wait_ge(D_pool, (t + 1) * D_POOLS)
                        dve.tensor_tensor(here, here, pq[:, 1, (k % 2) * 512:(k % 2) * 512 + D], ALU.add).then_inc(D_out, 1)
            dve.wait_ge(Q_pool, NT * Q_POOLS)
            group_loop(dve, ffn_step)


_INS = ["x", "adj", "nodemask", "L0_gnn_W", "L0_gnn_attn", "L1_gnn_h_target", "L1_gnn_ln1_scale", "L1_gnn_ln1_bias",
        "L1_gnn_Wq", "L1_gnn_bq", "L1_gnn_Wk", "L1_gnn_bk", "L1_gnn_Wv", "L1_gnn_bv", "L1_gnn_Wo", "L1_gnn_bo",
        "L1_gnn_ln2_scale", "L1_gnn_ln2_bias", "L1_gnn_W1", "L1_gnn_W2"]


def kernel(**inputs):
    import numpy as np
    import concourse.bacc as bacc
    from concourse.bass_utils import run_bass_kernel_spmd

    nc = bacc.Bacc("TRN2", target_bir_lowering=False, num_devices=1)
    arrays, args = {}, []
    for name in _INS:
        a = np.ascontiguousarray(inputs[name])
        arrays[f"in_{name}"] = a
        args.append(nc.dram_tensor(f"in_{name}", a.shape, mybir.dt.from_np(a.dtype), kind="ExternalInput").ap())
    args.append(nc.dram_tensor("out_x", (N, D), F32, kind="ExternalOutput").ap())
    build(nc, *args)
    r = run_bass_kernel_spmd(nc, [arrays], core_ids=[0])
    return r.results[0]["out_x"]
```

```python
from contextlib import ExitStack

import concourse.bass as bass
from concourse import mybir

ALU = mybir.AluOpType
ACT = mybir.ActivationFunctionType
F32 = mybir.dt.float32
F32R = mybir.dt.float32r
BF16 = mybir.dt.bfloat16
I32 = mybir.dt.int32

P = 128
N = 2048
D = 256
KC = D // P
NT = N // P
HEADS = 8
HD = D // HEADS
HPC = P // HD
HID = 4 * D
MC = HID // P
CH = 4
BLK = N // CH // P
HALF = N // 2
UNITS = NT * HEADS
GT = 4
NG = NT // GT
EPS = 1e-5
ALPHA = 0.2
MASKED = -float(2 ** 100)
LOWEST = -3.0e38
QSCALE = HD ** -0.5
VW = 2 * HD + 1


class Tile:

    def __init__(self, t=None, pair=None, parity=None):
        if isinstance(t, int):
            self.t, self.parity, self.pair = t, t % 2, t // 2
        else:
            self.parity, self.pair = parity, pair
            self.t = pair * 2 + parity
        self.static = isinstance(t, int)

    def ahead(self, k):
        if self.static:
            return Tile(self.t + k)
        n = self.parity + k
        return Tile(pair=self.pair + n // 2, parity=n % 2)

    def real(self):
        return not self.static or 0 <= self.t < NT


def tile_loop(eng, step, lead):
    last_pairs = (lead + 1) // 2
    for t in range(-lead, 2):
        step(Tile(t))
    with eng.Fori(1, NT // 2 - last_pairs) as pair:
        for parity in range(2):
            step(Tile(pair=pair, parity=parity))
    for t in range(NT - 2 * last_pairs, NT):
        step(Tile(t))


class Chain:

    def __init__(self, eng, sem, start):
        self.eng, self.sem, self.start, self.n = eng, sem, start, 0

    def link(self, ins, apart=None):
        self.n += 1
        ins.then_inc(self.sem, 1)
        if apart:
            apart(self.eng, (self.sem, self.start + self.n))
        else:
            self.eng.wait_ge(self.sem, self.start + self.n)

    def last(self, ins):
        self.n += 1
        ins.then_inc(self.sem, 1)


def build(nc, x, adj, nodemask, W0, attn0, h_target, ln1_scale, ln1_bias, Wq, bq, Wk, bk, Wv, bv, Wo, bo,
          ln2_scale, ln2_bias, W1, W2, out):
    ctx = ExitStack()
    with ctx:
        def sb(name, shape, dt=F32):
            return ctx.enter_context(nc.sbuf_tensor(name, shape, dt))

        def ps(name, shape):
            return ctx.enter_context(nc.psum_tensor(name, shape, F32))

        def sem(name):
            return ctx.enter_context(nc.semaphore(name))

        key_dram = nc.dram_tensor("key_split", (2, D, N), F32).ap()
        query_dram = nc.dram_tensor("query_split", (2, D, N), F32).ap()
        target_dram = nc.dram_tensor("target_normed", (N, D), F32).ap()
        residual_dram = nc.dram_tensor("residual_rows", (N, D), F32).ap()
        context_dram = nc.dram_tensor("context_rows", (N, D), F32).ap()

        ln1s, ln1b, ln2s, ln2b, bvr, bor = (sb(n, [P, D]) for n in ("ln1s", "ln1b", "ln2s", "ln2b", "bvr", "bor"))
        bqc, bkc = sb("bqc", [P, KC]), sb("bkc", [P, KC])
        node_i, node = sb("node_i", [P, NT], I32), sb("node", [P, NT])
        ident = sb("ident", [P, P])
        wo = sb("wo", [P, KC, D])
        fold = sb("fold", [VW, P])
        minus_half = sb("minus_half", [P, GT])
        mv, rstd = sb("mv", [P, GT, 2]), sb("rstd", [P, GT])
        stats = sb("stats", [P, GT, 6])
        normed = sb("normed", [P, 2, D])
        normedT = sb("normedT", [P, 2, KC, P])
        row1, row2, row3, affine = (sb(n, [P, D]) for n in ("row1", "row2", "row3", "affine"))
        rowmax, negmax = sb("rowmax", [P, 4, 2]), sb("negmax", [P, 4])
        recip = sb("recip", [P, HEADS])

        attention = ExitStack()

        def tmp(scope, name, shape, dt=F32):
            return scope.enter_context(nc.sbuf_tensor(name, shape, dt))

        key_stack = tmp(attention, "key_stack", [P, HEADS, N], F32R)
        value = tmp(attention, "value", [P, NT, HEADS, VW], F32R)
        adj_in = tmp(attention, "adj_in", [P, N], I32)
        whole = tmp(attention, "whole", [P, KC, P])
        part_a, part_b = tmp(attention, "part_a", [P, KC, P], F32R), tmp(attention, "part_b", [P, KC, P], F32R)

        wq = tmp(attention, "wq", [P, KC, D])
        target_in = tmp(attention, "target_in", [P, 2, D])

        graph = ExitStack()
        xres = tmp(graph, "xres", [P, NT, D])
        hproj = tmp(graph, "hproj", [P, NT, D + 1])
        src_row = tmp(graph, "src_row", [P, N])
        s1, s2 = tmp(graph, "s1", [P, NT]), tmp(graph, "s2", [P, 2])
        maskB = tmp(graph, "maskB", [P, N], BF16)
        scoresB = tmp(graph, "scoresB", [P, 2, N])
        w0 = scoresB[:, 0, 0:KC * D].rearrange("p (c n) -> p c n", c=KC)
        att = scoresB[:, 1, 0:2 * D].rearrange("p (c n) -> p c n", c=2)
        probsB = tmp(graph, "probsB", [P, CH, BLK * P])
        wk, wv = tmp(graph, "wk", [P, KC, D]), tmp(graph, "wv", [P, KC, D])
        vwhole = tmp(graph, "vwhole", [P, D])
        graph.close()

        heads = ExitStack()
        ring = tmp(heads, "ring", [P, 4, N])
        mask = tmp(heads, "mask", [P, 2, N], BF16)
        query_stack = tmp(heads, "query_stack", [P, 2, HEADS, P], F32R)
        probs_a, probs_b = (tmp(heads, n, [P, CH, BLK * P], F32R) for n in ("probs_a", "probs_b"))
        foldable = tmp(heads, "foldable", [VW, 2, P])
        unscaled = tmp(heads, "unscaled", [P, 2, HEADS, HD + 1])
        context = tmp(heads, "context", [P, 2, D])
        heads.close()
        attention.close()

        w1, w2 = sb("w1", [P, KC, HID]), sb("w2", [P, MC, D])
        hiddenT = sb("hiddenT", [P, MC, GT * P])
        postT = sb("postT", [P, KC, GT * P])
        post, ctx_rows, target_rows, res_rows = (sb(n, [P, GT, D]) for n in ("post", "ctx_rows", "target_rows", "res_rows"))
        post_in = sb("post_in", [P, GT, D])
        total = sb("total", [P, NT, D])

        pq = ps("pq", [P, 2, HALF])
        pt = ps("pt", [P, 2, BLK * P])
        pa = ps("pa", [P, 2, 512])

        def sems(names):
            return [sem(n) for n in names.split()]

        w0_in, small_in, ffn_in = sems("w0_in small_in ffn_in")
        ident_zeroed, ident_made, fold_made, ones_made, node_made, bq_scaled = sems(
            "ident_zeroed ident_made fold_made ones_made node_made bq_scaled")
        x_in = [sem(f"x_in{g}") for g in range(NT // GT)]
        A_step, A_roots, A_normed, A_transposed, A_reluT, A_projected, A_copied, A_scored, A_rowed, A_rowcopied = sems(
            "A_step A_roots A_normed A_transposed A_reluT A_projected A_copied A_scored A_rowed A_rowcopied")
        adjB_in, B_masked, B_scored, B_leaky, B_max, B_neg, B_probs, B_T, B_evac, B_av = sems(
            "adjB_in B_masked B_scored B_leaky B_max B_neg B_probs B_T B_evac B_av")
        B_step, B_expneg, B_roots, B_affine, B_hsT, B_hsTcopied, B_projK, B_projV, B_whole, B_vwhole, B_parts = sems(
            "B_step B_expneg B_roots B_affine B_hsT B_hsTcopied B_projK B_projV B_whole B_vwhole B_parts")
        key_split_out, key_stacked, residual_out = sems("key_split_out key_stacked residual_out")
        Q_step, Q_roots, Q_affine, Q_parts, Q_T, Q_Tcopied, Q_proj, Q_whole, query_split_out, targets_out = sems(
            "Q_step Q_roots Q_affine Q_parts Q_T Q_Tcopied Q_proj Q_whole query_split_out targets_out")
        target_in_sem = [sem(f"target_in{i}") for i in range(2)]
        query_stacked = [sem(f"query_stacked{i}") for i in range(2)]
        adjC_in, C_masked, C_qk, C_max, C_neg, C_probs, C_T, C_a, C_b, C_av, C_foldable, C_folded, C_unscaled = sems(
            "adjC_in C_masked C_qk C_max C_neg C_probs C_T C_a C_b C_av C_foldable C_folded C_unscaled")
        C_recip, C_ctx, C_biased, context_out = sems("C_recip C_ctx C_biased context_out")
        ctx_rows_in, target_rows_in, res_rows_in = sems("ctx_rows_in target_rows_in res_rows_in")
        D_ctxT, D_ctxTcopied, D_attn, D_step, D_roots, D_affine, D_total, D_postT, D_postTcopied, D_hidden, D_gelu, D_ff, D_out, stored = sems(
            "D_ctxT D_ctxTcopied D_attn D_step D_roots D_affine D_total D_postT D_postTcopied D_hidden D_gelu D_ff D_out stored")
        B_STEPS, B_AFFINES, B_PARTS, Q_STEPS, Q_AFFINES, Q_PARTS = 14, 3, 4, 4, 3, 2
        D_STEPS = 5 * GT + 1
        SMALL = 13 * 16

        def rows(dram, t):
            return dram[bass.ds(t * P, P), :]

        def cols(t):
            return bass.ds(t * P, P)

        def slot(tensor, t):
            return tensor[:, bass.ds(t, 1), 0:D].rearrange("p t d -> p (t d)")

        def flat(tensor):
            return tensor.rearrange("p c n -> p (c n)")

        def split_rows(dram, part, t):
            return dram[part, :, cols(t)].rearrange("(c p) n -> p c n", p=P)

        def stack_rows(dram, part, t):
            return dram[part, :, cols(t)].rearrange("(h d) n -> d h n", d=HD)

        def after(eng, s, value):
            if not isinstance(value, int) or value > 0:
                eng.wait_ge(s, value)

        def apart(eng, *waits):
            waits = [(s, v if isinstance(v, int) else eng.compute_val(v)) for s, v in waits if not isinstance(v, int) or v > 0]
            if waits:
                eng.wait_ge(ident_made, 1)
            for s, value in waits:
                eng.wait_ge(s, value)

        def row_stats(eng, chain, src):
            chain.link(eng.bn_stats(stats[:, 0, :], src), apart)
            chain.link(eng.bn_aggr(mv[:, 0, :], stats[:, 0, :]))
            chain.last(eng.tensor_scalar(mv[:, 0, 1:2], mv[:, 0, 1:2], EPS, None, ALU.add))

        def normalise(eng, dst, src, roots, root):
            eng.wait_ge(roots, root)
            return eng.tensor_scalar(dst, src, mv[:, 0, 0:1], rstd[:, 0:1], ALU.subtract, ALU.mult)

        def inverse_root(pool, steps, step, roots):
            pool.wait_ge(steps, step)
            pool.tensor_tensor(rstd[:, 0:1], mv[:, 0, 1:2], minus_half[:, 0:1], ALU.pow).then_inc(roots, 1)

        def unit(v, h):
            u = v.ahead(h // HEADS)
            return u, h % HEADS, u.t * HEADS + h % HEADS

        def chunk_ahead(v, h, c):
            u, hu, n = unit(v, h + (1 if c < 2 else 2))
            cu = (c + 2) % CH
            return u, hu, cu, n * CH + cu

        def group_loop(eng, step):
            step(-1)
            step(0)
            with eng.Fori(1, NG - 1) as g:
                step(g)
            step(NG - 1)

        def attention_over(eng):
            eng.wait_ge(B_av, NT * CH)
            eng.wait_ge(B_max, NT)
            eng.wait_ge(B_step, NT * B_STEPS)
            eng.wait_ge(B_parts, NT * B_PARTS)
            eng.wait_ge(B_projV, NT)
            eng.wait_ge(residual_out, NT * 16)

        block = ctx.enter_context(nc.Block())

        @block.sync
        def _(sp):
            xv = x.rearrange("(g t p) d -> g p t d", p=P, t=GT)
            sp.dma_start(xres[:, 0:GT, :], xv[0]).then_inc(x_in[0], 16)
            sp.dma_start(w0, W0.rearrange("(c p) n -> p c n", p=P)).then_inc(w0_in, 16)
            for i in range(2):
                sp.dma_start(att[:, i, :], attn0[i * D:(i + 1) * D, :].rearrange("d o -> o d").broadcast_to([P, D])).then_inc(w0_in, 16)
            for g in range(1, NT // GT):
                sp.dma_start(xres[:, GT * g:GT * g + GT, :], xv[g]).then_inc(x_in[g], 16)
            for dst, w in ((wk, Wk), (wv, Wv), (wo, Wo), (wq, Wq)):
                sp.dma_start(dst[:], w.rearrange("(c p) n -> p c n", p=P)).then_inc(small_in, 16)
            for dst, v in ((ln1s, ln1_scale), (ln1b, ln1_bias), (ln2s, ln2_scale), (ln2b, ln2_bias), (bvr, bv), (bor, bo)):
                sp.dma_start(dst[:], v.rearrange("(a d) -> a d", a=1).broadcast_to([P, D])).then_inc(small_in, 16)
            with nc.allow_non_contiguous_dma(reason="a few thousand single values, once"):
                for dst, v in ((bqc, bq), (bkc, bk), (node_i, nodemask)):
                    sp.dma_start(dst[:], v.rearrange("(c p) -> p c", p=P)).then_inc(small_in, 16)
            sp.dma_start(target_in[:, 0, :], h_target[0:P, :]).then_inc(target_in_sem[0], 16)

            def gat_step(v):
                u = v.ahead(4)
                if u.real():
                    apart(sp, (B_masked, u.t))
                    sp.dma_start(adj_in[:], rows(adj, u.t)).then_inc(adjB_in, 16)
                if v.real():
                    apart(sp, (B_step, v.t * B_STEPS + 5))
                    sp.dma_start(rows(residual_dram, v.t), slot(xres, v.t)).then_inc(residual_out, 16)
                    apart(sp, (B_parts, v.t * B_PARTS + 2))
                    sp.dma_start(split_rows(key_dram, 0, v.t), part_a[:].bitcast(F32)).then_inc(key_split_out, 16)
                    sp.dma_start(split_rows(key_dram, 1, v.t), part_b[:].bitcast(F32)).then_inc(key_split_out, 16)
                    apart(sp, (key_split_out, v.t * 32 + 32))
                    for r, part in enumerate((0, 1, 0, 1)):
                        sp.dma_start(key_stack[r * HD:(r + 1) * HD, :, cols(v.t)].bitcast(F32), stack_rows(key_dram, part, v.t)).then_inc(key_stacked, 16)
            tile_loop(sp, gat_step, 4)

            def mha_step(v):
                u = v.ahead(2)
                if u.real():
                    if not (u.static and u.t == 0):
                        apart(sp, (Q_step, (u.t - 1) * Q_STEPS))
                        sp.dma_start(target_in[:, u.parity, :], rows(h_target, u.t)).then_inc(target_in_sem[u.parity], 16)
                    if u.static and u.t == 0:
                        sp.wait_ge(B_masked, NT)
                    apart(sp, (C_masked, u.t))
                    sp.dma_start(adj_in[:], rows(adj, u.t)).then_inc(adjC_in, 16)
                u = v.ahead(1)
                if u.real():
                    apart(sp, (Q_affine, (u.t + 1) * Q_AFFINES))
                    sp.dma_start(rows(target_dram, u.t), normed[:, u.parity, :]).then_inc(targets_out, 16)
                    apart(sp, (Q_parts, (u.t + 1) * Q_PARTS))
                    sp.dma_start(split_rows(query_dram, 0, u.t), part_a[:].bitcast(F32)).then_inc(query_split_out, 16)
                    sp.dma_start(split_rows(query_dram, 1, u.t), part_b[:].bitcast(F32)).then_inc(query_split_out, 16)
                    apart(sp, (query_split_out, u.t * 32 + 32))
                    apart(sp, (C_qk, (u.t - 1) * HEADS * 2))
                    for r, part in enumerate((0, 0, 1, 1)):
                        sp.dma_start(query_stack[r * HD:(r + 1) * HD, u.parity, :, :].bitcast(F32), stack_rows(query_dram, part, u.t)).then_inc(query_stacked[u.parity], 16)
                if v.real():
                    apart(sp, (C_biased, v.t + 1))
                    sp.dma_start(rows(context_dram, v.t), context[:, v.parity, :]).then_inc(context_out, 16)
            attention_over(sp)
            tile_loop(sp, mha_step, 2)

            sp.wait_ge(C_qk, UNITS * 2)
            sp.dma_start(w1[:], W1.rearrange("(c p) n -> p c n", p=P)).then_inc(ffn_in, 16)
            sp.dma_start(w2[:], W2.rearrange("(c p) n -> p c n", p=P)).then_inc(ffn_in, 16)
            sp.wait_ge(targets_out, NT * 16)
            sp.wait_ge(residual_out, NT * 16)
            sp.wait_ge(context_out, NT * 16)

            def group(dram, g):
                return dram[bass.ds(g * GT * P, GT * P), :].rearrange("(t p) d -> p t d", p=P)

            def ffn_step(v):
                if not isinstance(v, int) or v + 1 < NG:
                    apart(sp, (D_ctxT, (v + 1) * GT), (D_affine, (v + 1) * GT * 3), (D_total, (v + 1) * GT))
                    sp.dma_start(ctx_rows[:], group(context_dram, v + 1)).then_inc(ctx_rows_in, 16)
                    sp.dma_start(target_rows[:], group(target_dram, v + 1)).then_inc(target_rows_in, 16)
                    sp.dma_start(res_rows[:], group(residual_dram, v + 1)).then_inc(res_rows_in, 16)
                if not isinstance(v, int) or v >= 0:
                    apart(sp, (D_out, (v + 1) * GT))
                    sp.dma_start(group(out, v), total[:, bass.ds(v * GT, GT), :]).then_inc(stored, 16)
            group_loop(sp, ffn_step)
            sp.wait_ge(stored, NG * 16)

        @block.gpsimd
        def _(pool):
            pool.memset(ident[:], 0.0).then_inc(ident_zeroed, 1)
            pool.memset(fold[:], 0.0).then_inc(ident_zeroed, 1)
            pool.wait_ge(ident_zeroed, 2)
            pool.affine_select(out=ident[:], in_=ident[:], compare_op=ALU.not_equal, fill=1.0, base=0,
                               pattern=[[-1, P]], channel_multiplier=1).then_inc(ident_made, 1)
            pool.affine_select(out=fold[:], in_=fold[:], compare_op=ALU.not_equal, fill=1.0, base=0,
                               pattern=[[-1, P]], channel_multiplier=1).then_inc(fold_made, 1)
            pool.wait_ge(fold_made, 1)
            pool.affine_select(out=fold[:], in_=fold[:], compare_op=ALU.not_equal, fill=1.0, base=-(HD + 1),
                               pattern=[[-1, P]], channel_multiplier=1).then_inc(fold_made, 1)
            pool.memset(minus_half[:], -0.5).then_inc(ones_made, 1)
            pool.memset(hproj[:, :, D:D + 1], 1.0).then_inc(ones_made, 1)
            pool.memset(value[:, :, :, HD:HD + 1].bitcast(F32), 1.0).then_inc(ones_made, 1)
            pool.wait_ge(ones_made, 3)

            def root_step(v):
                if v.ahead(2).real():
                    inverse_root(pool, A_step, (v.ahead(2).t + 1) * 3, A_roots)
            tile_loop(pool, root_step, 2)
            pool.wait_ge(small_in, SMALL)
            pool.tensor_scalar(node[:], node_i[:], 1, None, ALU.is_equal).then_inc(node_made, 1)
            pool.tensor_scalar(bqc[:], bqc[:], QSCALE, None, ALU.mult).then_inc(bq_scaled, 1)
            pool.wait_ge(node_made, 1)
            pool.wait_ge(A_transposed, NT)

            def affine_rows(chain, dst, scale, bias, t):
                chain.link(pool.tensor_tensor(affine[:], row3[:], scale[:], ALU.mult))
                chain.link(pool.tensor_tensor(affine[:], affine[:], bias[:], ALU.add))
                return pool.tensor_tensor(dst, affine[:], node[:, bass.ds(t, 1)].broadcast_to([P, D]), ALU.mult)

            def gat_step(v):
                e = v.ahead(1)
                if e.real():
                    inverse_root(pool, B_step, e.t * B_STEPS + 8, B_roots)
                    inverse_root(pool, B_step, e.t * B_STEPS + 13, B_roots)
                    chain = Chain(pool, B_affine, e.t * B_AFFINES)
                    pool.wait_ge(B_step, (e.t + 1) * B_STEPS)
                    after(pool, B_hsT, e.t - 1)
                    chain.link(affine_rows(chain, normed[:, e.parity, :], ln1s, ln1b, e.t))
                if v.real():
                    chain = Chain(pool, B_parts, v.t * B_PARTS)
                    apart(pool, (B_whole, (v.t + 1) * KC), (key_split_out, v.t * 32))
                    chain.link(pool.tensor_copy(part_a[:], whole[:]))
                    chain.link(pool.tensor_tensor(part_b[:], whole[:], part_a[:].bitcast(F32), ALU.subtract))
                    here = value[:, bass.ds(v.t, 1), :, :].rearrange("p t h d -> p (t h) d")
                    values = vwhole[:, :].rearrange("p (h d) -> p h d", d=HD)
                    apart(pool, (B_vwhole, v.t + 1))
                    chain.link(pool.tensor_copy(here[:, :, 0:HD], values))
                    chain.link(pool.tensor_tensor(here[:, :, HD + 1:VW], values, here[:, :, 0:HD].bitcast(F32), ALU.subtract))
            tile_loop(pool, gat_step, 3)

            def mha_step(v):
                u = v.ahead(1)
                if u.real():
                    chain = Chain(pool, Q_parts, u.t * Q_PARTS)
                    apart(pool, (Q_whole, (u.t + 1) * KC), (query_split_out, u.t * 32))
                    chain.link(pool.tensor_copy(part_a[:], whole[:]))
                    chain.link(pool.tensor_tensor(part_b[:], whole[:], part_a[:].bitcast(F32), ALU.subtract))
                u = v.ahead(2)
                if u.real():
                    apart(pool, (adjC_in, (u.t + 1) * 16), (C_max, (u.t - 1) * HEADS * 2))
                    pool.tensor_scalar(mask[:, u.parity, :], adj_in[:], 0, MASKED, ALU.is_equal, ALU.mult).then_inc(C_masked, 1)
                    inverse_root(pool, Q_step, u.t * Q_STEPS + 3, Q_roots)
                    chain = Chain(pool, Q_affine, u.t * Q_AFFINES)
                    pool.wait_ge(Q_step, (u.t + 1) * Q_STEPS)
                    after(pool, Q_T, u.t - 1)
                    after(pool, targets_out, (u.t - 1) * 16)
                    chain.link(affine_rows(chain, normed[:, u.parity, :], ln1s, ln1b, u.t))
                if v.real():
                    pool.wait_ge(C_ctx, v.t + 1)
                    pool.tensor_tensor(context[:, v.parity, :], context[:, v.parity, :], bvr[:], ALU.add).then_inc(C_biased, 1)
            attention_over(pool)
            pool.wait_ge(B_hsT, NT)
            tile_loop(pool, mha_step, 2)

            def ffn_step(v):
                if isinstance(v, int) and v + 1 >= NG:
                    return
                g = v + 1
                pool.wait_ge(D_step, g * D_STEPS + 4 * GT + 1)
                pool.tensor_tensor(rstd[:], mv[:, :, 1:2].rearrange("p k o -> p (k o)"), minus_half[:], ALU.pow).then_inc(D_roots, 1)
                pool.wait_ge(res_rows_in, (g + 1) * 16)
                for k in range(GT):
                    t = g * GT + k
                    row = target_rows[:, k, :]
                    chain = Chain(pool, D_affine, t * 3)
                    pool.wait_ge(D_step, g * D_STEPS + 4 * GT + 2 + k)
                    chain.link(pool.tensor_tensor(row, row, ln2s[:], ALU.mult))
                    chain.link(pool.tensor_tensor(row, row, ln2b[:], ALU.add))
                    after(pool, D_postT, g * GT - (GT - 1) + k)
                    chain.link(pool.tensor_tensor(post[:, k, :], row, node[:, bass.ds(t, 1)].broadcast_to([P, D]), ALU.mult))
                    pool.tensor_tensor(slot(total, t), res_rows[:, k, :], post[:, k, :], ALU.add).then_inc(D_total, 1)
            pool.wait_ge(C_av, UNITS * CH)
            group_loop(pool, ffn_step)

        @block.tensor
        def _(pe):
            def transposes(dst, src, ready):
                for k in range(KC):
                    last = pe.transpose(dst[:, k * P:(k + 1) * P], src[:, k * P:(k + 1) * P], ident[:])
                last.then_inc(ready, 1)

            def project(dst, lhsT, w, ready):
                for c in range(KC):
                    last = pe.matmul(dst, lhsT[:, c, :], w[:, c, :], start=(c == 0), stop=(c == KC - 1))
                last.then_inc(ready, 1)

            def project_heads(dst, w, rhsT, ready):
                for m in range(KC):
                    for c in range(KC):
                        last = pe.matmul(dst[:, m * P:(m + 1) * P], w[:, c, m * P:(m + 1) * P], rhsT[:, c, :],
                                         start=(c == 0), stop=(c == KC - 1))
                last.then_inc(ready, 1)

            def proj_step(v):
                if v.real():
                    pe.wait_ge(A_scored, (v.t + 1) * 2)
                    after(pe, A_rowcopied, v.t - 1)
                    pe.matmul(pa[:, v.parity, 0:P], s2[:, v.parity:v.parity + 1].broadcast_to([P, P]), ident[:],
                              start=True, stop=True).then_inc(A_rowed, 1)
                u = v.ahead(1)
                if u.real():
                    pe.wait_ge(A_reluT, u.t + 1)
                    after(pe, A_copied, u.t - 1)
                    project(pq[:, u.parity, 0:D], normedT[:, u.parity], w0, A_projected)
                u = v.ahead(2)
                if u.real():
                    pe.wait_ge(A_normed, u.t + 1)
                    after(pe, A_reluT, u.t - 1)
                    transposes(pt[:, u.parity, :], normed[:, u.parity, :], A_transposed)
            pe.wait_ge(ident_made, 1)
            pe.wait_ge(w0_in, 48)
            tile_loop(pe, proj_step, 2)

            def gat_step(v):
                u = v.ahead(2)

                def turn(c):
                    if c == 0:
                        pe.wait_ge(B_probs, u.t + 1)
                    after(pe, B_evac, u.t * CH + c - 1)
                    for k in range(BLK):
                        last = pe.transpose(pt[:, c % 2, k * P:(k + 1) * P],
                                            scoresB[:, u.parity, (c * BLK + k) * P:(c * BLK + k + 1) * P], ident[:])
                    last.then_inc(B_T, 1)

                def weigh(c):
                    pe.wait_ge(B_evac, u.t * CH + c + 1)
                    if c == 0:
                        after(pe, B_step, (u.t - 2) * B_STEPS + 2)
                    for k in range(BLK):
                        last = pe.matmul(pa[:, u.parity, 0:D + 1], probsB[:, c, k * P:(k + 1) * P], hproj[:, c * BLK + k, :],
                                         start=(c + k == 0), stop=(c == CH - 1 and k == BLK - 1))
                    last.then_inc(B_av, 1)

                if u.real():
                    turn(0)
                    turn(1)
                    weigh(0)
                    turn(2)
                    weigh(1)
                if v.real():
                    pe.wait_ge(B_affine, (v.t + 1) * B_AFFINES)
                    after(pe, B_hsTcopied, v.t)
                    transposes(pq[:, 0, 0:D], normed[:, v.parity, :], B_hsT)
                if u.real():
                    turn(3)
                    weigh(2)
                if v.real():
                    pe.wait_ge(B_hsTcopied, v.t + 1)
                    after(pe, B_whole, v.t * KC)
                    project_heads(pq[:, 0, 512:512 + D], wk, normedT[:, 0], B_projK)
                    after(pe, B_vwhole, v.t)
                    project(pq[:, 1, 0:D], normedT[:, 0], wv, B_projV)
                if u.real():
                    weigh(3)
            pe.wait_ge(A_reluT, NT)
            pe.wait_ge(A_copied, NT)
            pe.wait_ge(A_rowcopied, NT)
            pe.wait_ge(ones_made, 3)
            pe.wait_ge(small_in, SMALL)
            tile_loop(pe, gat_step, 3)

            def mha_step(v):
                for h in range(HEADS):
                    uq, hq, nq = unit(v, h + 4)
                    ua, ha, na = unit(v, h + 1)
                    n = v.t * HEADS + h
                    for c in range(CH):
                        if uq.real() and c % 2 == 0:
                            half = c // 2
                            if hq == 0 and half == 0:
                                pe.wait_ge(query_stacked[uq.parity], (uq.pair + 1) * 64)
                            after(pe, C_max, nq * 2 + half - 1)
                            for k in range(2):
                                at = half * HALF + k * 512
                                last = pe.matmul(pq[:, half, k * 512:(k + 1) * 512], query_stack[:, uq.parity, hq, :],
                                                 key_stack[:, hq, at:at + 512], start=True, stop=True)
                            last.then_inc(C_qk, 1)
                        ut, ht, ct, m = chunk_ahead(v, h, c)
                        if ut.real():
                            if ct % 2 == 0:
                                pe.wait_ge(C_probs, m // 2 + 1 if isinstance(m, int) else (ut.t * HEADS + ht) * 2 + ct // 2 + 1)
                            after(pe, C_b, m - 1)
                            for k in range(BLK):
                                last = pe.transpose(pt[:, ct % 2, k * P:(k + 1) * P],
                                                    ring[:, ht % 4, (ct * BLK + k) * P:(ct * BLK + k + 1) * P], ident[:])
                            last.then_inc(C_T, 1)
                        if ua.real():
                            if c == 0:
                                after(pe, C_unscaled, na - 1)
                                if h == 1 and ua.real():
                                    pe.wait_ge(Q_Tcopied, v_ahead_count(v))
                                if h == 2 and ua.real():
                                    pe.wait_ge(Q_whole, v_ahead_count(v) * KC)
                            pe.wait_ge(C_b, na * CH + c + 1)
                            for k in range(BLK):
                                for part in (probs_a, probs_b):
                                    last = pe.matmul(pa[0:VW, ha % 2, 0:P], value[:, c * BLK + k, ha, :], part[:, c, k * P:(k + 1) * P],
                                                     start=(c + k == 0 and part is probs_a),
                                                     stop=(c == CH - 1 and k == BLK - 1 and part is probs_b))
                            last.then_inc(C_av, 1)
                        if v.real() and c == 1:
                            pe.wait_ge(C_foldable, n + 1)
                            pe.matmul(pa[:, h % 2, P:2 * P], foldable[:, h % 2, :], fold[:], start=True, stop=True).then_inc(C_folded, 1)
                        u = v.ahead(1)
                        if u.real() and v.real() and h < 2 and c == 2:
                            pe.wait_ge(C_unscaled, n + 1)
                        if u.real() and h == 0 and c == 2:
                            pe.wait_ge(Q_affine, (u.t + 1) * Q_AFFINES)
                            transposes(pa[:, 0, 2 * P:4 * P], normed[:, u.parity, :], Q_T)
                        if u.real() and h == 1 and c == 2:
                            pe.wait_ge(Q_Tcopied, u.t + 1)
                            project_heads(pa[:, 1, 2 * P:4 * P], wq, normedT[:, 0], Q_proj)

            def v_ahead_count(v):
                return min(v.t + 2, NT) if v.static else v.t + 2

            pe.wait_ge(B_hsTcopied, NT)
            pe.wait_ge(B_whole, NT * KC)
            pe.wait_ge(B_vwhole, NT)
            pe.wait_ge(B_parts, NT * B_PARTS)
            pe.wait_ge(B_evac, NT * CH)
            pe.wait_ge(B_step, NT * B_STEPS)
            pe.wait_ge(fold_made, 2)
            pe.wait_ge(key_stacked, NT * 64)
            tile_loop(pe, mha_step, 2)

            def ffn_step(v):
                ahead = not isinstance(v, int) or v + 1 < NG
                now = not isinstance(v, int) or v >= 0
                if ahead:
                    pe.wait_ge(ctx_rows_in, (v + 2) * 16)
                    for k in range(GT + 1):
                        t = (v + 1) * GT + k
                        if k < GT:
                            after(pe, D_ctxTcopied, t - 1)
                            after(pe, D_postTcopied, (v + 1) * GT)
                            transposes(pt[:, k % 2, :], ctx_rows[:, k, :], D_ctxT)
                        if k:
                            t = t - 1
                            pe.wait_ge(D_ctxTcopied, t + 1)
                            if k > 2:
                                pe.wait_ge(D_step, (v + 1) * D_STEPS + k - 2)
                            else:
                                after(pe, D_step, (v + 1) * D_STEPS)
                            project(pa[:, (k - 1) % 2, 0:D], normedT[:, (k - 1) % 2], wo, D_attn)
                if now:
                    pe.wait_ge(D_postTcopied, (v + 1) * GT)
                    for m in range(MC):
                        n = v * MC + m
                        if not (isinstance(n, int) and n < 2):
                            if m < 2:
                                after(pe, D_gelu, v * MC)
                            else:
                                after(pe, D_gelu, n - 1)
                        for c in range(KC):
                            last = pe.matmul(pq[:, 0, (m % 2) * 512:(m % 2 + 1) * 512], w1[:, c, m * P:(m + 1) * P], postT[:, c, :],
                                             start=(c == 0), stop=(c == KC - 1))
                        last.then_inc(D_hidden, 1)
                for k in range(GT):
                    if ahead:
                        t = (v + 1) * GT + k
                        pe.wait_ge(D_affine, (t + 1) * 3)
                        after(pe, D_ctxTcopied, (v + 2) * GT)
                        if k >= 2:
                            after(pe, D_postTcopied, t - 1)
                        transposes(pt[:, k % 2, :], post[:, k, :], D_postT)
                    if now:
                        t = v * GT + k
                        if k == 0:
                            pe.wait_ge(D_gelu, (v + 1) * MC)
                        if k < 2:
                            after(pe, D_out, v * GT)
                        else:
                            after(pe, D_out, t - 1)
                        for m in range(MC):
                            last = pe.matmul(pq[:, 1, (k % 2) * 512:(k % 2) * 512 + D], hiddenT[:, m, k * P:(k + 1) * P], w2[:, m, :],
                                             start=(m == 0), stop=(m == MC - 1))
                        last.then_inc(D_ff, 1)
            pe.wait_ge(Q_whole, NT * KC)
            pe.wait_ge(C_unscaled, UNITS)
            pe.wait_ge(C_max, UNITS * 2)
            pe.wait_ge(C_b, UNITS * CH)
            pe.wait_ge(ffn_in, 32)
            group_loop(pe, ffn_step)

        @block.scalar
        def _(act):
            def proj_step(v):
                if v.real():
                    act.wait_ge(A_rowed, v.t + 1)
                    act.copy(src_row[:, cols(v.t)], pa[:, v.parity, 0:P]).then_inc(A_rowcopied, 1)
                u = v.ahead(1)
                if u.real():
                    act.wait_ge(A_projected, u.t + 1)
                    act.copy(slot(hproj, u.t), pq[:, u.parity, 0:D]).then_inc(A_copied, 1)
                u = v.ahead(2)
                if u.real():
                    act.wait_ge(A_transposed, u.t + 1)
                    after(act, A_projected, u.t - 1)
                    act.activation(flat(normedT[:, u.parity]), pt[:, u.parity, 0:D], ACT.Relu).then_inc(A_reluT, 1)
            tile_loop(act, proj_step, 2)

            def gat_step(v):
                u = v.ahead(2)

                def evacuate(c):
                    act.wait_ge(B_T, u.t * CH + c + 1)
                    after(act, B_av, u.t * CH + c - 3)
                    act.copy(probsB[:, c, :], pt[:, c % 2, :]).then_inc(B_evac, 1)

                if u.real():
                    evacuate(0)
                    evacuate(1)
                e = v.ahead(1)
                if e.real():
                    act.wait_ge(B_step, e.t * B_STEPS + 3)
                    act.activation(row2[:], row2[:], ACT.Exp).then_inc(B_expneg, 1)
                if u.real():
                    evacuate(2)
                if v.real():
                    act.wait_ge(B_hsT, v.t + 1)
                    after(act, B_projV, v.t)
                    act.copy(flat(normedT[:, 0]), pq[:, 0, 0:D]).then_inc(B_hsTcopied, 1)
                if u.real():
                    evacuate(3)
                if v.real():
                    act.wait_ge(B_projK, v.t + 1)
                    after(act, B_parts, (v.t - 1) * B_PARTS + 2)
                    for c in range(KC):
                        act.activation(whole[:, c, :], pq[:, 0, 512 + c * P:512 + (c + 1) * P], ACT.Identity, bias=bkc[:, c:c + 1],
                                       scale=1.0).then_inc(B_whole, 1)
                    act.wait_ge(B_projV, v.t + 1)
                    after(act, B_parts, v.t * B_PARTS)
                    act.copy(vwhole[:], pq[:, 1, 0:D]).then_inc(B_vwhole, 1)
                w = v.ahead(3)
                if w.real():
                    act.wait_ge(B_neg, w.t + 1)
                    act.activation(scoresB[:, w.parity, :], scoresB[:, w.parity, :], ACT.Exp, bias=negmax[:, w.parity:w.parity + 1],
                                   scale=1.0).then_inc(B_probs, 1)
                w = v.ahead(4)
                if w.real():
                    after(act, B_T, (w.t - 1) * CH)
                    act.activation(scoresB[:, w.parity, :], src_row[:], ACT.Identity, bias=s1[:, bass.ds(w.t, 1)],
                                   scale=1.0).then_inc(B_scored, 1)
            act.wait_ge(A_rowcopied, NT)
            act.wait_ge(A_scored, NT * 2)
            act.wait_ge(A_projected, NT)
            act.wait_ge(small_in, SMALL)
            tile_loop(act, gat_step, 4)

            def mha_step(v):
                for h in range(HEADS):
                    ue, he, ne = unit(v, h + 3)
                    n = v.t * HEADS + h

                    def part_a_of(c):
                        ut, ht, ct, m = chunk_ahead(v, h, c)
                        if ut.real():
                            act.wait_ge(C_T, m + 1)
                            after(act, C_av, m - 3)
                            act.copy(probs_a[:, ct, :], pt[:, ct % 2, :]).then_inc(C_a, 1)

                    def exponentiate(half):
                        if ue.real():
                            if half == 0:
                                act.wait_ge(C_neg, ne + 1)
                            here = ring[:, he % 4, half * HALF:(half + 1) * HALF]
                            act.activation(here, here, ACT.Exp, bias=negmax[:, he % 4:he % 4 + 1], scale=1.0).then_inc(C_probs, 1)

                    if v.real():
                        act.wait_ge(C_av, (n + 1) * CH)
                        after(act, C_folded, n - 1)
                        act.copy(foldable[:, h % 2, :], pa[0:VW, h % 2, 0:P]).then_inc(C_foldable, 1)
                    part_a_of(0)
                    exponentiate(0)
                    part_a_of(1)
                    if v.real():
                        act.wait_ge(C_folded, n + 1)
                        if h == 0:
                            after(act, C_ctx, v.t - 1)
                        act.copy(unscaled[:, v.parity, h, :], pa[:, h % 2, P:P + HD + 1]).then_inc(C_unscaled, 1)
                    part_a_of(2)
                    exponentiate(1)
                    u = v.ahead(1)
                    if u.real() and h == 0:
                        act.wait_ge(Q_T, u.t + 1)
                        after(act, Q_proj, u.t)
                        act.copy(flat(normedT[:, 0]), pa[:, 0, 2 * P:4 * P]).then_inc(Q_Tcopied, 1)
                    if u.real() and h == 1:
                        act.wait_ge(Q_proj, u.t + 1)
                        after(act, Q_parts, u.t * Q_PARTS)
                        for c in range(KC):
                            act.activation(whole[:, c, :], pa[:, 1, (2 + c) * P:(3 + c) * P], ACT.Identity, bias=bqc[:, c:c + 1],
                                           scale=QSCALE).then_inc(Q_whole, 1)
                    part_a_of(3)
            attention_over(act)
            act.wait_ge(bq_scaled, 1)
            tile_loop(act, mha_step, 2)

            def ffn_step(v):
                ahead = not isinstance(v, int) or v + 1 < NG
                now = not isinstance(v, int) or v >= 0
                if ahead:
                    for k in range(GT):
                        t = (v + 1) * GT + k
                        act.wait_ge(D_ctxT, t + 1)
                        after(act, D_attn, t - 1)
                        act.copy(flat(normedT[:, k % 2]), pt[:, k % 2, 0:D]).then_inc(D_ctxTcopied, 1)
                if now:
                    after(act, D_ff, v * GT)
                    for m in range(MC):
                        act.wait_ge(D_hidden, v * MC + m + 1)
                        act.activation(hiddenT[:, m, :], pq[:, 0, (m % 2) * 512:(m % 2 + 1) * 512], ACT.Gelu_apprx_tanh).then_inc(D_gelu, 1)
                if ahead:
                    for k in range(GT):
                        t = (v + 1) * GT + k
                        act.wait_ge(D_postT, t + 1)
                        after(act, D_hidden, (v + 1) * MC)
                        act.copy(postT[:, :, k * P:(k + 1) * P], pt[:, k % 2, 0:D].rearrange("p (c n) -> p c n", n=P)).then_inc(D_postTcopied, 1)
            act.wait_ge(C_av, UNITS * CH)
            act.wait_ge(Q_proj, NT)
            group_loop(act, ffn_step)

        @block.vector
        def _(dve):
            def proj_step(v):
                u = v.ahead(2)
                if u.real():
                    chain = Chain(dve, A_step, u.t * 3)
                    if u.static:
                        dve.wait_ge(x_in[u.t // GT], 16)
                    apart(dve, (A_transposed, u.t - 1))
                    row_stats(dve, chain, slot(xres, u.t))
                e = v.ahead(1)
                if e.real():
                    dve.wait_ge(A_copied, e.t + 1)
                    after(dve, A_rowed, e.t - 1)
                    after(dve, A_scored, e.t * 2)
                    dve.scalar_tensor_tensor(out=row1[:], in0=slot(hproj, e.t), scalar=1.0, in1=att[:, 0, :], op0=ALU.mult, op1=ALU.mult,
                                             accum_out=s1[:, bass.ds(e.t, 1)]).then_inc(A_scored, 1)
                    dve.scalar_tensor_tensor(out=row2[:], in0=slot(hproj, e.t), scalar=1.0, in1=att[:, 1, :], op0=ALU.mult, op1=ALU.mult,
                                             accum_out=s2[:, e.parity:e.parity + 1]).then_inc(A_scored, 1)
                if u.real():
                    normalise(dve, normed[:, u.parity, :], slot(xres, u.t), A_roots, u.t + 1).then_inc(A_normed, 1)
            dve.wait_ge(w0_in, 48)
            for g in range(NT // GT):
                dve.wait_ge(x_in[g], 16)
            tile_loop(dve, proj_step, 2)

            def gat_step(v):
                e, w = v.ahead(1), v.ahead(3)
                chain = Chain(dve, B_step, e.t * B_STEPS)
                s = scoresB[:, w.parity, :]
                if e.real():
                    dve.wait_ge(B_av, (e.t + 1) * CH)
                    chain.link(dve.reciprocal(recip[:, 0:1], pa[:, e.parity, D:D + 1]))
                    chain.link(dve.tensor_scalar(row1[:], pa[:, e.parity, 0:D], recip[:, 0:1], None, ALU.mult))
                    chain.link(dve.tensor_scalar(row2[:], row1[:], 0.0, None, ALU.min))
                if w.real():
                    dve.wait_ge(B_scored, w.t + 1)
                    dve.scalar_tensor_tensor(out=s, in0=s, scalar=ALPHA, in1=s, op0=ALU.mult, op1=ALU.max).then_inc(B_leaky, 1)
                if e.real():
                    dve.wait_ge(B_expneg, e.t + 1)
                    chain.link(dve.scalar_tensor_tensor(out=row1[:], in0=row2[:], scalar=-1.0, in1=row1[:], op0=ALU.add, op1=ALU.max))
                    chain.link(dve.tensor_tensor(slot(xres, e.t), slot(xres, e.t), row1[:], ALU.add), apart)
                    row_stats(dve, chain, slot(xres, e.t))
                if w.real():
                    dve.wait_ge(adjB_in, (w.t + 1) * 16)
                    after(dve, B_max, w.t)
                    dve.tensor_scalar(maskB[:], adj_in[:], 0, MASKED, ALU.is_le, ALU.mult).then_inc(B_masked, 1)
                if e.real():
                    chain.link(normalise(dve, row1[:], slot(xres, e.t), B_roots, e.t * 2 + 1))
                    chain.link(dve.tensor_scalar(row1[:], row1[:], 0.0, None, ALU.max), apart)
                    row_stats(dve, chain, row1[:])
                if w.real():
                    apart(dve, (B_leaky, w.t + 1), (B_masked, w.t + 1))
                    dve.tensor_tensor_reduce(s, s, maskB[:], 1.0, LOWEST, ALU.add, ALU.max,
                                             rowmax[:, w.parity, 0:1]).then_inc(B_max, 1)
                if e.real():
                    after(dve, B_affine, e.t * B_AFFINES)
                    chain.last(normalise(dve, row3[:], row1[:], B_roots, e.t * 2 + 2))
                    assert chain.n == B_STEPS
                if w.real():
                    dve.wait_ge(B_max, w.t + 1)
                    dve.tensor_scalar(negmax[:, w.parity:w.parity + 1], rowmax[:, w.parity, 0:1], -1.0, None, ALU.mult).then_inc(B_neg, 1)
            dve.wait_ge(A_scored, NT * 2)
            tile_loop(dve, gat_step, 3)

            def mha_step(v):
                for h in range(HEADS):
                    um, hm, nm = unit(v, h + 4)

                    def part_b_of(c):
                        ut, ht, ct, m = chunk_ahead(v, h, c)
                        if ut.real():
                            dve.wait_ge(C_a, m + 1)
                            after(dve, C_av, m - 3)
                            dve.tensor_tensor(probs_b[:, ct, :], pt[:, ct % 2, :], probs_a[:, ct, :].bitcast(F32),
                                              ALU.subtract).then_inc(C_b, 1)

                    def mask_and_max(half):
                        if um.real():
                            if hm == 0 and half == 0:
                                dve.wait_ge(C_masked, um.t + 1)
                            if half == 0:
                                after(dve, C_T, (nm - 3) * CH)
                            apart(dve, (C_qk, nm * 2 + half + 1))
                            at = slice(half * HALF, (half + 1) * HALF)
                            dve.tensor_tensor_reduce(ring[:, hm % 4, at], pq[:, half, :], mask[:, um.parity, at], 1.0, LOWEST,
                                                     ALU.add, ALU.max, rowmax[:, hm % 4, half:half + 1]).then_inc(C_max, 1)

                    part_b_of(0)
                    mask_and_max(0)
                    part_b_of(1)
                    part_b_of(2)
                    mask_and_max(1)
                    part_b_of(3)
                    if um.real():
                        dve.wait_ge(C_max, nm * 2 + 2)
                        dve.tensor_reduce(negmax[:, hm % 4:hm % 4 + 1], rowmax[:, hm % 4, :], mybir.AxisListType.X, ALU.max,
                                          negate=True).then_inc(C_neg, 1)
                    u = v.ahead(2)
                    if u.real() and h == 5:
                        apart(dve, (target_in_sem[u.parity], (u.pair + 1) * 16))
                        row_stats(dve, Chain(dve, Q_step, u.t * Q_STEPS), target_in[:, u.parity, :])
                    if u.real() and h == 7:
                        after(dve, Q_affine, u.t * Q_AFFINES)
                        normalise(dve, row3[:], target_in[:, u.parity, :], Q_roots, u.t + 1).then_inc(Q_step, 1)
                if v.real():
                    here = unscaled[:, v.parity]
                    dve.wait_ge(C_unscaled, (v.t + 1) * HEADS)
                    dve.reciprocal(recip[:, :].rearrange("p (h o) -> p h o", o=1), here[:, :, HD:HD + 1]).then_inc(C_recip, 1)
                    dve.wait_ge(C_recip, v.t + 1)
                    after(dve, context_out, (v.t - 1) * 16)
                    dve.tensor_tensor(context[:, v.parity, :].rearrange("p (h d) -> p h d", d=HD), here[:, :, 0:HD],
                                      recip[:, :].rearrange("p (h o) -> p h o", o=1).broadcast_to([P, HEADS, HD]), ALU.mult).then_inc(C_ctx, 1)
            attention_over(dve)
            tile_loop(dve, mha_step, 2)

            def ffn_step(v):
                ahead = not isinstance(v, int) or v + 1 < NG
                now = not isinstance(v, int) or v >= 0
                if ahead:
                    g = v + 1
                    base = g * D_STEPS
                    dve.wait_ge(target_rows_in, (g + 1) * 16)
                    for k in range(GT):
                        dve.wait_ge(D_attn, g * GT + k + 1)
                        dve.tensor_tensor(post_in[:, k, :], pa[:, k % 2, 0:D], bor[:], ALU.add).then_inc(D_step, 1)
                    for k in range(GT):
                        dve.wait_ge(D_step, base + k + 1)
                        dve.scalar_tensor_tensor(out=target_rows[:, k, :], in0=post_in[:, k, :], scalar=node[:, bass.ds(g * GT + k, 1)],
                                                 in1=target_rows[:, k, :], op0=ALU.mult, op1=ALU.add).then_inc(D_step, 1)
                    for k in range(GT):
                        apart(dve, (D_step, base + GT + k + 1))
                        dve.bn_stats(stats[:, k, :], target_rows[:, k, :]).then_inc(D_step, 1)
                    for k in range(GT):
                        apart(dve, (D_step, base + 2 * GT + k + 1))
                        dve.bn_aggr(mv[:, k, :], stats[:, k, :]).then_inc(D_step, 1)
                    dve.wait_ge(D_step, base + 4 * GT)
                    dve.tensor_scalar(mv[:, :, 1:2], mv[:, :, 1:2], EPS, None, ALU.add).then_inc(D_step, 1)
                    dve.wait_ge(D_roots, g + 1)
                    for k in range(GT):
                        dve.tensor_scalar(target_rows[:, k, :], target_rows[:, k, :], mv[:, k, 0:1], rstd[:, k:k + 1],
                                          ALU.subtract, ALU.mult).then_inc(D_step, 1)
                if now:
                    for k in range(GT):
                        t = v * GT + k
                        dve.wait_ge(D_ff, t + 1)
                        dve.wait_ge(D_total, t + 1)
                        dve.tensor_tensor(slot(total, t), slot(total, t), pq[:, 1, (k % 2) * 512:(k % 2) * 512 + D],
                                          ALU.add).then_inc(D_out, 1)
            group_loop(dve, ffn_step)


_INS = ["x", "adj", "nodemask", "L0_gnn_W", "L0_gnn_attn", "L1_gnn_h_target", "L1_gnn_ln1_scale", "L1_gnn_ln1_bias",
        "L1_gnn_Wq", "L1_gnn_bq", "L1_gnn_Wk", "L1_gnn_bk", "L1_gnn_Wv", "L1_gnn_bv", "L1_gnn_Wo", "L1_gnn_bo",
        "L1_gnn_ln2_scale", "L1_gnn_ln2_bias", "L1_gnn_W1", "L1_gnn_W2"]


def kernel(**inputs):
    import numpy as np
    import concourse.bacc as bacc
    from concourse.bass_utils import run_bass_kernel_spmd

    nc = bacc.Bacc("TRN2", target_bir_lowering=False, num_devices=1)
    arrays, args = {}, []
    for name in _INS:
        a = np.ascontiguousarray(inputs[name])
        arrays[f"in_{name}"] = a
        args.append(nc.dram_tensor(f"in_{name}", a.shape, mybir.dt.from_np(a.dtype), kind="ExternalInput").ap())
    args.append(nc.dram_tensor("out_x", (N, D), F32, kind="ExternalOutput").ap())
    build(nc, *args)
    r = run_bass_kernel_spmd(nc, [arrays], core_ids=[0])
    return r.results[0]["out_x"]
```

```python
from contextlib import ExitStack

import concourse.bass as bass
from concourse import mybir

ALU = mybir.AluOpType
ACT = mybir.ActivationFunctionType
F32 = mybir.dt.float32
F32R = mybir.dt.float32r
BF16 = mybir.dt.bfloat16
I32 = mybir.dt.int32

P = 128
N = 2048
D = 256
KC = D // P
NT = N // P
HEADS = 8
HD = D // HEADS
HPC = P // HD
HID = 4 * D
MC = HID // P
CH = 4
BLK = N // CH // P
HALF = N // 2
UNITS = NT * HEADS
GT = 4
NG = NT // GT
EPS = 1e-5
ALPHA = 0.2
MASKED = float(2 ** 100)
HIGHEST = 3.0e38
QSCALE = HD ** -0.5
VW = 2 * HD + 1


class Tile:

    def __init__(self, t=None, pair=None, parity=None):
        if isinstance(t, int):
            self.t, self.parity, self.pair = t, t % 2, t // 2
        else:
            self.parity, self.pair = parity, pair
            self.t = pair * 2 + parity
        self.static = isinstance(t, int)

    def ahead(self, k):
        if self.static:
            return Tile(self.t + k)
        n = self.parity + k
        return Tile(pair=self.pair + n // 2, parity=n % 2)

    def real(self):
        return not self.static or 0 <= self.t < NT


def tile_loop(eng, step, lead):
    last_pairs = (lead + 1) // 2
    for t in range(-lead, 2):
        step(Tile(t))
    with eng.Fori(1, NT // 2 - last_pairs) as pair:
        for parity in range(2):
            step(Tile(pair=pair, parity=parity))
    for t in range(NT - 2 * last_pairs, NT):
        step(Tile(t))


class Chain:

    def __init__(self, eng, sem, start):
        self.eng, self.sem, self.start, self.n = eng, sem, start, 0

    def link(self, ins, apart=None):
        self.n += 1
        ins.then_inc(self.sem, 1)
        if apart:
            apart(self.eng, (self.sem, self.start + self.n))
        else:
            self.eng.wait_ge(self.sem, self.start + self.n)

    def last(self, ins):
        self.n += 1
        ins.then_inc(self.sem, 1)


def build(nc, x, adj, nodemask, W0, attn0, h_target, ln1_scale, ln1_bias, Wq, bq, Wk, bk, Wv, bv, Wo, bo,
          ln2_scale, ln2_bias, W1, W2, out):
    ctx = ExitStack()
    with ctx:
        def sb(name, shape, dt=F32):
            return ctx.enter_context(nc.sbuf_tensor(name, shape, dt))

        def ps(name, shape):
            return ctx.enter_context(nc.psum_tensor(name, shape, F32))

        def sem(name):
            return ctx.enter_context(nc.semaphore(name))

        key_dram = nc.dram_tensor("key_split", (2, D, N), F32).ap()
        query_dram = nc.dram_tensor("query_split", (2, D, N), F32).ap()
        target_dram = nc.dram_tensor("target_normed", (N, D), F32).ap()
        residual_dram = nc.dram_tensor("residual_rows", (N, D), F32).ap()
        context_dram = nc.dram_tensor("context_rows", (N, D), F32).ap()

        ln1s, ln1b, ln2s, ln2b, bvr, bor = (sb(n, [P, D]) for n in ("ln1s", "ln1b", "ln2s", "ln2b", "bvr", "bor"))
        bqc, bkc = sb("bqc", [P, KC]), sb("bkc", [P, KC])
        node_i, node = sb("node_i", [P, NT], I32), sb("node", [P, NT])
        ident = sb("ident", [P, P])
        minus_half = sb("minus_half", [P, GT])
        mv, rstd = sb("mv", [P, GT, 2]), sb("rstd", [P, GT])
        stats = sb("stats", [P, GT, 6])
        normed = sb("normed", [P, 2, D])
        normedT = sb("normedT", [P, 2, KC, P])
        row1, row2, row3, affine = (sb(n, [P, D]) for n in ("row1", "row2", "row3", "affine"))
        least = sb("least", [P, 4, 2])
        recip = sb("recip", [P, HEADS])

        attention = ExitStack()

        def tmp(scope, name, shape, dt=F32):
            return scope.enter_context(nc.sbuf_tensor(name, shape, dt))

        key_stack = tmp(attention, "key_stack", [P, HEADS, N], F32R)
        query_stack = tmp(attention, "query_stack", [P, 2, HEADS, P], F32R)
        value = tmp(attention, "value", [P, NT, HEADS, VW], F32R)
        adj_in = tmp(attention, "adj_in", [P, N], I32)
        whole = tmp(attention, "whole", [P, KC, P])
        part_a, part_b = tmp(attention, "part_a", [P, KC, P], F32R), tmp(attention, "part_b", [P, KC, P], F32R)
        wq = tmp(attention, "wq", [P, KC, D])
        target_in = tmp(attention, "target_in", [P, 2, D])

        graph = ExitStack()
        xres = tmp(graph, "xres", [P, NT, D])
        hproj = tmp(graph, "hproj", [P, NT, D + 1])
        src_row = tmp(graph, "src_row", [P, N])
        s1, s2 = tmp(graph, "s1", [P, NT]), tmp(graph, "s2", [P, 2])
        maskB = tmp(graph, "maskB", [P, N], BF16)
        scoresB = tmp(graph, "scoresB", [P, 2, N])
        w0 = scoresB[:, 0, 0:KC * (D + 2)].rearrange("p (c n) -> p c n", c=KC)
        att = scoresB[:, 1, 0:2 * D].rearrange("p (c n) -> p c n", c=2)
        probsB = tmp(graph, "probsB", [P, CH, BLK * P])
        wk, wv = tmp(graph, "wk", [P, KC, D]), tmp(graph, "wv", [P, KC, D])
        vwhole = tmp(graph, "vwhole", [P, D])
        graph.close()

        heads = ExitStack()
        ring = tmp(heads, "ring", [P, 4, N])
        mask = tmp(heads, "mask", [P, 2, N], BF16)
        probs_a, probs_b = (tmp(heads, n, [P, CH, BLK * P], F32R) for n in ("probs_a", "probs_b"))
        raw = tmp(heads, "raw", [P, BLK * P])
        contextT = tmp(heads, "contextT", [VW, 2, P])
        unscaled = tmp(heads, "unscaled", [P, 2, HEADS, VW])
        context = tmp(heads, "context", [P, 2, D])
        heads.close()
        attention.close()

        wo = sb("wo", [P, KC, D])
        w1, w2 = sb("w1", [P, KC, HID]), sb("w2", [P, MC, D])
        hiddenT = sb("hiddenT", [P, MC, GT * P])
        postT = sb("postT", [P, KC, GT * P])
        post, ctx_rows, target_rows, res_rows = (sb(n, [P, GT, D]) for n in ("post", "ctx_rows", "target_rows", "res_rows"))
        total = sb("total", [P, NT, D])

        pq = ps("pq", [P, 2, HALF])
        pt = ps("pt", [P, 2, BLK * P])
        pa = ps("pa", [P, 2, 512])

        def sems(names):
            return [sem(n) for n in names.split()]

        w0_in, small_in, wo_in, ffn_in = sems("w0_in small_in wo_in ffn_in")
        ident_zeroed, ident_made, ones_made, node_made, bq_scaled = sems(
            "ident_zeroed ident_made ones_made node_made bq_scaled")
        x_in = [sem(f"x_in{g}") for g in range(NT // GT)]
        A_weights = sem("A_weights")
        A_step, A_roots, A_normed, A_transposed, A_reluT, A_projected, A_copied, A_scored, A_rowed, A_rowcopied = sems(
            "A_step A_roots A_normed A_transposed A_reluT A_projected A_copied A_scored A_rowed A_rowcopied")
        adjB_in, B_masked, B_scored, B_leaky, B_least, B_probs, B_T, B_evac, B_av = sems(
            "adjB_in B_masked B_scored B_leaky B_least B_probs B_T B_evac B_av")
        B_step, B_expneg, B_roots, B_affine, B_hsT, B_hsTcopied, B_projK, B_projV, B_whole, B_vwhole, B_parts = sems(
            "B_step B_expneg B_roots B_affine B_hsT B_hsTcopied B_projK B_projV B_whole B_vwhole B_parts")
        key_split_out, key_stacked, residual_out = sems("key_split_out key_stacked residual_out")
        Q_step, Q_roots, Q_affine, Q_parts, Q_T, Q_Tcopied, Q_proj, Q_whole, query_split_out, targets_out = sems(
            "Q_step Q_roots Q_affine Q_parts Q_T Q_Tcopied Q_proj Q_whole query_split_out targets_out")
        target_in_sem = [sem(f"target_in{i}") for i in range(2)]
        query_stacked = [sem(f"query_stacked{i}") for i in range(2)]
        adjC_in, C_masked, C_qk, C_least, C_probs, C_T, C_a, C_b, C_av, C_contextT, C_turned, C_unscaled = sems(
            "adjC_in C_masked C_qk C_least C_probs C_T C_a C_b C_av C_contextT C_turned C_unscaled")
        C_raw, C_pool_b = sems("C_raw C_pool_b")
        C_recip, C_ctx, C_biased, context_out = sems("C_recip C_ctx C_biased context_out")
        ctx_rows_in, target_rows_in, res_rows_in = sems("ctx_rows_in target_rows_in res_rows_in")
        D_ctxT, D_ctxTcopied, D_attn, D_step, D_roots, D_post, D_total, D_postT, D_postTcopied, D_hidden, D_gelu, D_ff, D_out, stored = sems(
            "D_ctxT D_ctxTcopied D_attn D_step D_roots D_post D_total D_postT D_postTcopied D_hidden D_gelu D_ff D_out stored")
        B_STEPS, B_AFFINES, B_PARTS, Q_STEPS, Q_AFFINES, Q_PARTS = 14, 3, 4, 4, 3, 2
        D_STEPS = 5 * GT + 2
        SMALL = 12 * 16
        PIECES = 8

        def rows(dram, t):
            return dram[bass.ds(t * P, P), :]

        def cols(t):
            return bass.ds(t * P, P)

        def slot(tensor, t):
            return tensor[:, bass.ds(t, 1), 0:D].rearrange("p t d -> p (t d)")

        def flat(tensor):
            return tensor.rearrange("p c n -> p (c n)")

        def split_rows(dram, part, t):
            return dram[part, :, cols(t)].rearrange("(c p) n -> p c n", p=P)

        def stack_rows(dram, part, t):
            return dram[part, :, cols(t)].rearrange("(h d) n -> d h n", d=HD)

        def after(eng, s, value):
            if not isinstance(value, int) or value > 0:
                eng.wait_ge(s, value)

        def apart(eng, *waits):
            waits = [(s, v if isinstance(v, int) else eng.compute_val(v)) for s, v in waits if not isinstance(v, int) or v > 0]
            if waits:
                eng.wait_ge(ident_made, 1)
            for s, value in waits:
                eng.wait_ge(s, value)

        def row_stats(eng, chain, src, k=0):
            chain.link(eng.bn_stats(stats[:, k, :], src), apart)
            chain.link(eng.bn_aggr(mv[:, k, :], stats[:, k, :]))
            chain.last(eng.tensor_scalar(mv[:, k, 1:2], mv[:, k, 1:2], EPS, None, ALU.add))

        def normalise(eng, dst, src, roots, root, k=0):
            eng.wait_ge(roots, root)
            return eng.tensor_scalar(dst, src, mv[:, k, 0:1], rstd[:, k:k + 1], ALU.subtract, ALU.mult)

        def inverse_root(pool, steps, step, roots, k=0):
            pool.wait_ge(steps, step)
            pool.tensor_tensor(rstd[:, k:k + 1], mv[:, k, 1:2], minus_half[:, 0:1], ALU.pow).then_inc(roots, 1)

        def unit(v, h):
            u = v.ahead(h // HEADS)
            return u, h % HEADS, u.t * HEADS + h % HEADS

        def chunk_ahead(v, h, c):
            u, hu, n = unit(v, h + (1 if c < 2 else 2))
            cu = (c + 2) % CH
            return u, hu, cu, n * CH + cu

        def group_loop(eng, step, last=1):
            step(0)
            with eng.Fori(1, NG - last) as g:
                step(g)
            for g in range(NG - last, NG):
                step(g)

        def attention_over(eng):
            eng.wait_ge(B_av, NT * CH)
            eng.wait_ge(B_least, NT)
            eng.wait_ge(B_step, NT * B_STEPS)
            eng.wait_ge(B_parts, NT * B_PARTS)
            eng.wait_ge(B_projV, NT)
            eng.wait_ge(residual_out, NT * 16)

        def later_tile(u):
            return u.real() and not (u.static and u.t == 0)

        def by_pool(h, c):
            return h % 2 == 1 and c == CH - 1

        def wait_parts(eng, u, h, c):
            if by_pool(h, c):
                after(eng, C_pool_b, u.t * (HEADS // 2) + h // 2 + 1)
            else:
                after(eng, C_b, u.t * (HEADS * CH - HEADS // 2) + h // 2 * (2 * CH - 1) + h % 2 * CH + c + 1)

        def wait_slot(eng, u, h, c):
            h, c = (h, c - 2) if c >= 2 else (h - 1, c + 2)
            if by_pool(h, c):
                after(eng, C_a, (u.t * HEADS + h) * CH + c + 1)
            else:
                wait_parts(eng, u, h, c)

        def front_place(v, h):
            return v.static and v.t == NT - 1 and h == 5

        block = ctx.enter_context(nc.Block())

        @block.sync
        def _(sp):
            xv = x.rearrange("(g t p) d -> g p t d", p=P, t=GT)
            sp.dma_start(xres[:, 0:GT, :], xv[0]).then_inc(x_in[0], 16)
            sp.dma_start(w0[:, :, 0:D], W0.rearrange("(c p) n -> p c n", p=P)).then_inc(w0_in, 16)
            for i in range(2):
                sp.dma_start(att[:, i, :], attn0[i * D:(i + 1) * D, :].rearrange("d o -> o d").broadcast_to([P, D])).then_inc(w0_in, 16)
            for g in range(1, NT // GT):
                sp.dma_start(xres[:, GT * g:GT * g + GT, :], xv[g]).then_inc(x_in[g], 16)
            sp.dma_start(adj_in[:], rows(adj, 0)).then_inc(adjB_in, 16)
            for dst, w in ((wk, Wk), (wv, Wv), (wq, Wq)):
                sp.dma_start(dst[:], w.rearrange("(c p) n -> p c n", p=P)).then_inc(small_in, 16)
            for dst, v in ((ln1s, ln1_scale), (ln1b, ln1_bias), (ln2s, ln2_scale), (ln2b, ln2_bias), (bvr, bv), (bor, bo)):
                sp.dma_start(dst[:], v.rearrange("(a d) -> a d", a=1).broadcast_to([P, D])).then_inc(small_in, 16)
            with nc.allow_non_contiguous_dma(reason="a few thousand single values, once"):
                for dst, v in ((bqc, bq), (bkc, bk), (node_i, nodemask)):
                    sp.dma_start(dst[:], v.rearrange("(c p) -> p c", p=P)).then_inc(small_in, 16)
            sp.dma_start(target_in[:, 0, :], h_target[0:P, :]).then_inc(target_in_sem[0], 16)

            def store_queries(u):
                apart(sp, (Q_affine, (u.t + 1) * Q_AFFINES))
                sp.dma_start(rows(target_dram, u.t), normed[:, u.parity, :]).then_inc(targets_out, 16)
                apart(sp, (Q_parts, (u.t + 1) * Q_PARTS))
                sp.dma_start(split_rows(query_dram, 0, u.t), part_a[:].bitcast(F32)).then_inc(query_split_out, 16)
                sp.dma_start(split_rows(query_dram, 1, u.t), part_b[:].bitcast(F32)).then_inc(query_split_out, 16)
                apart(sp, (query_split_out, u.t * 32 + 32))

            def stack_queries(u):
                for r, part in enumerate((0, 0, 1, 1)):
                    sp.dma_start(query_stack[r * HD:(r + 1) * HD, u.parity, :, :].bitcast(F32), stack_rows(query_dram, part, u.t)).then_inc(query_stacked[u.parity], 16)

            def gat_step(v):
                if v.static and v.t == -4:
                    store_queries(Tile(0))
                    stack_queries(Tile(0))
                if v.static and v.t == NT - 2:
                    sp.wait_ge(B_masked, NT)
                    sp.dma_start(adj_in[:], rows(adj, 0)).then_inc(adjC_in, 16)
                    sp.dma_start(target_in[:, 1, :], rows(h_target, 1)).then_inc(target_in_sem[1], 16)
                if v.real():
                    apart(sp, (B_step, v.t * B_STEPS + 5))
                    sp.dma_start(rows(residual_dram, v.t), slot(xres, v.t)).then_inc(residual_out, 16)
                    apart(sp, (B_parts, v.t * B_PARTS + 2))
                    sp.dma_start(split_rows(key_dram, 0, v.t), part_a[:].bitcast(F32)).then_inc(key_split_out, 16)
                    sp.dma_start(split_rows(key_dram, 1, v.t), part_b[:].bitcast(F32)).then_inc(key_split_out, 16)
                    apart(sp, (key_split_out, v.t * 32 + 32), (key_stacked, v.t * 64))
                    for r, part in enumerate((0, 1, 0, 1)):
                        sp.dma_start(key_stack[r * HD:(r + 1) * HD, :, cols(v.t)].bitcast(F32), stack_rows(key_dram, part, v.t)).then_inc(key_stacked, 16)
            tile_loop(sp, gat_step, 4)

            def mha_step(v):
                u = v.ahead(2)
                if later_tile(u):
                    if not (u.static and u.t == 1):
                        apart(sp, (Q_step, (u.t - 1) * Q_STEPS))
                        sp.dma_start(target_in[:, u.parity, :], rows(h_target, u.t)).then_inc(target_in_sem[u.parity], 16)
                u = v.ahead(1)
                if later_tile(u):
                    store_queries(u)
                    apart(sp, (C_qk, (u.t - 1) * HEADS * 2))
                    stack_queries(u)
                u = v.ahead(2)
                if later_tile(u):
                    apart(sp, (C_masked, u.t * PIECES))
                    sp.dma_start(adj_in[:], rows(adj, u.t)).then_inc(adjC_in, 16)
                if v.static and v.t == NT - 1:
                    sp.wait_ge(targets_out, NT * 16)
                    sp.wait_ge(residual_out, NT * 16)
                    sp.wait_ge(context_out, (NT - 1) * 16)
                    sp.wait_ge(C_qk, UNITS * 2)
                    sp.dma_start(wo[:], Wo.rearrange("(c p) n -> p c n", p=P)).then_inc(wo_in, 16)
                    load_rows(0)
                    sp.dma_start(w1[:], W1.rearrange("(c p) n -> p c n", p=P)).then_inc(ffn_in, 16)
                    sp.dma_start(w2[:], W2.rearrange("(c p) n -> p c n", p=P)).then_inc(ffn_in, 16)
                    load_rows(1)
                if v.real():
                    apart(sp, (C_biased, v.t + 1))
                    sp.dma_start(rows(context_dram, v.t), context[:, v.parity, :]).then_inc(context_out, 16)

            def group(dram, g):
                return dram[bass.ds(g * GT * P, GT * P), :].rearrange("(t p) d -> p t d", p=P)

            def load_rows(g):
                apart(sp, (D_ctxT, g * GT))
                sp.dma_start(ctx_rows[:], group(context_dram, g)).then_inc(ctx_rows_in, 16)
                apart(sp, (D_post, g * GT))
                sp.dma_start(target_rows[:], group(target_dram, g)).then_inc(target_rows_in, 16)
                apart(sp, (D_total, g * GT))
                sp.dma_start(res_rows[:], group(residual_dram, g)).then_inc(res_rows_in, 16)
            tile_loop(sp, mha_step, 2)
            sp.wait_ge(context_out, NT * 16)

            def ffn_step(g):
                if not isinstance(g, int) or g + 2 < NG:
                    load_rows(g + 2)
                if not isinstance(g, int) or g + 1 < NG:
                    apart(sp, (D_out, (g + 1) * GT))
                    sp.dma_start(group(out, g), total[:, bass.ds(g * GT, GT), :]).then_inc(stored, 16)
                else:
                    for t in range(g * GT, (g + 1) * GT):
                        sp.wait_ge(D_out, t + 1)
                        sp.dma_start(rows(out, t), total[:, t, :]).then_inc(stored, 16)
            group_loop(sp, ffn_step, 2)
            sp.wait_ge(stored, (NG - 1 + GT) * 16)

        @block.gpsimd
        def _(pool):
            pool.memset(ident[:], 0.0).then_inc(ident_zeroed, 1)
            pool.wait_ge(ident_zeroed, 1)
            pool.affine_select(out=ident[:], in_=ident[:], compare_op=ALU.not_equal, fill=1.0, base=0,
                               pattern=[[-1, P]], channel_multiplier=1).then_inc(ident_made, 1)
            pool.memset(minus_half[:], -0.5).then_inc(ones_made, 1)
            pool.memset(hproj[:, :, D:D + 1], 1.0).then_inc(ones_made, 1)
            pool.memset(value[:, :, :, HD:HD + 1].bitcast(F32), 1.0).then_inc(ones_made, 1)
            pool.wait_ge(ones_made, 3)

            def root_step(v):
                u = v.ahead(5)
                if u.real():
                    inverse_root(pool, A_step, (u.t + 1) * 3, A_roots, u.parity)
            tile_loop(pool, root_step, 5)
            pool.wait_ge(small_in, SMALL)
            pool.tensor_scalar(node[:], node_i[:], 1, None, ALU.is_equal).then_inc(node_made, 1)
            pool.tensor_scalar(bqc[:], bqc[:], -QSCALE, None, ALU.mult).then_inc(bq_scaled, 1)
            pool.wait_ge(node_made, 1)
            pool.wait_ge(A_transposed, NT)

            def affine_rows(chain, dst, scale, bias, t):
                chain.link(pool.tensor_tensor(affine[:], row3[:], scale[:], ALU.mult))
                chain.link(pool.tensor_tensor(affine[:], affine[:], bias[:], ALU.add))
                return pool.tensor_tensor(dst, affine[:], node[:, bass.ds(t, 1)].broadcast_to([P, D]), ALU.mult)

            def target_root(u):
                inverse_root(pool, Q_step, u.t * Q_STEPS + 3, Q_roots)

            def affine_targets(u):
                chain = Chain(pool, Q_affine, u.t * Q_AFFINES)
                pool.wait_ge(Q_step, (u.t + 1) * Q_STEPS)
                after(pool, Q_T, u.t - 1)
                after(pool, targets_out, (u.t - 1) * 16)
                chain.last(affine_rows(chain, normed[:, u.parity, :], ln1s, ln1b, u.t))

            def query_parts(u):
                chain = Chain(pool, Q_parts, u.t * Q_PARTS)
                apart(pool, (Q_whole, (u.t + 1) * KC), (query_split_out, u.t * 32))
                chain.link(pool.tensor_copy(part_a[:], whole[:]))
                chain.last(pool.tensor_tensor(part_b[:], whole[:], part_a[:].bitcast(F32), ALU.subtract))

            target_root(Tile(0))
            affine_targets(Tile(0))
            pool.wait_ge(bq_scaled, 1)
            query_parts(Tile(0))
            pool.wait_ge(Q_T, 1)
            pool.wait_ge(targets_out, 16)
            pool.wait_ge(query_split_out, 32)

            def value_parts(v):
                chain = Chain(pool, B_parts, v.t * B_PARTS + 2)
                here = value[:, bass.ds(v.t, 1), :, :].rearrange("p t h d -> p (t h) d")
                values = vwhole[:, :].rearrange("p (h d) -> p h d", d=HD)
                apart(pool, (B_vwhole, v.t + 1))
                chain.link(pool.tensor_copy(here[:, :, 0:HD], values))
                chain.last(pool.tensor_tensor(here[:, :, HD + 1:VW], values, here[:, :, 0:HD].bitcast(F32), ALU.subtract))

            def gat_step(v):
                e = v.ahead(1)
                if e.real():
                    inverse_root(pool, B_step, e.t * B_STEPS + 8, B_roots)
                if v.ahead(-1).real():
                    value_parts(v.ahead(-1))
                if e.real():
                    inverse_root(pool, B_step, e.t * B_STEPS + 13, B_roots)
                    chain = Chain(pool, B_affine, e.t * B_AFFINES)
                    pool.wait_ge(B_step, (e.t + 1) * B_STEPS)
                    after(pool, B_hsT, e.t - 1)
                    chain.last(affine_rows(chain, normed[:, e.parity, :], ln1s, ln1b, e.t))
                if v.real():
                    chain = Chain(pool, B_parts, v.t * B_PARTS)
                    apart(pool, (B_whole, (v.t + 1) * KC), (key_split_out, v.t * 32))
                    chain.link(pool.tensor_copy(part_a[:], whole[:]))
                    chain.link(pool.tensor_tensor(part_b[:], whole[:], part_a[:].bitcast(F32), ALU.subtract))
            tile_loop(pool, gat_step, 3)
            value_parts(Tile(NT - 1))

            def front(g):
                pool.wait_ge(D_step, g * D_STEPS + 3 * GT + 2)
                pool.tensor_tensor(rstd[:], mv[:, :, 1:2].rearrange("p k o -> p (k o)"), minus_half[:], ALU.pow).then_inc(D_roots, 1)
                pool.wait_ge(res_rows_in, (g + 1) * 16)
                for k in range(GT):
                    t = g * GT + k
                    pool.wait_ge(D_post, t + 1)
                    pool.tensor_tensor(slot(total, t), res_rows[:, k, :], post[:, k, :], ALU.add).then_inc(D_total, 1)

            def mask_piece(u, piece):
                if not later_tile(u):
                    return
                if u.static and u.t == 1 and piece == 0:
                    attention_over(pool)
                if piece == 0:
                    apart(pool, (adjC_in, (u.t + 1) * 16), (C_least, (u.t - 1) * HEADS * 2))
                at = slice(piece * N // PIECES, (piece + 1) * N // PIECES)
                pool.tensor_scalar(mask[:, u.parity, at], adj_in[:, at], 0, MASKED, ALU.is_equal, ALU.mult).then_inc(C_masked, 1)

            def split(v, h):
                if v.real():
                    pool.wait_ge(C_raw, v.t * (HEADS // 2) + h // 2 + 1)
                    pool.wait_ge(C_a, (v.t * HEADS + h + 1) * CH)
                    pool.tensor_tensor(probs_b[:, CH - 1, :], raw[:], probs_a[:, CH - 1, :].bitcast(F32), ALU.subtract).then_inc(C_pool_b, 1)

            def finish_context(v):
                pool.wait_ge(C_recip, v.t + 1)
                after(pool, context_out, (v.t - 1) * 16)
                here = context[:, v.parity, :].rearrange("p (h d) -> p h d", d=HD)
                chain = Chain(pool, C_ctx, v.t * 2)
                chain.link(pool.tensor_tensor(here, unscaled[:, v.parity, :, 0:HD], unscaled[:, v.parity, :, HD + 1:VW], ALU.add))
                chain.link(pool.tensor_tensor(here, here, recip[:, :].rearrange("p (h o) -> p h o", o=1).broadcast_to([P, HEADS, HD]), ALU.mult))
                pool.tensor_tensor(context[:, v.parity, :], context[:, v.parity, :], bvr[:], ALU.add).then_inc(C_biased, 1)

            def mha_step(v):
                before, one, two = v.ahead(-1), v.ahead(1), v.ahead(2)
                split(v, 1)
                if before.real():
                    finish_context(before)
                mask_piece(one, 3)
                mask_piece(one, 4)
                mask_piece(one, 5)
                if later_tile(one):
                    query_parts(one)
                split(v, 3)
                mask_piece(one, 6)
                mask_piece(one, 7)
                split(v, 5)
                if later_tile(two):
                    target_root(two)
                mask_piece(two, 0)
                split(v, 7)
                mask_piece(two, 1)
                mask_piece(two, 2)
                if later_tile(two):
                    affine_targets(two)
                if front_place(v, 5):
                    front(0)
            pool.wait_ge(B_hsT, NT)
            pool.wait_ge(key_split_out, NT * 32)

            tile_loop(pool, mha_step, 2)
            finish_context(Tile(NT - 1))

            def ffn_step(v):
                if not isinstance(v, int) or v + 1 < NG:
                    front(v + 1)
            group_loop(pool, ffn_step)

        @block.tensor
        def _(pe):
            def transposes(dst, src, ready):
                for k in range(KC):
                    last = pe.transpose(dst[:, k * P:(k + 1) * P], src[:, k * P:(k + 1) * P], ident[:])
                last.then_inc(ready, 1)

            def project(dst, lhsT, w, ready):
                for c in range(KC):
                    last = pe.matmul(dst, lhsT[:, c, :], w[:, c, :], start=(c == 0), stop=(c == KC - 1))
                last.then_inc(ready, 1)

            def project_heads(dst, w, rhsT, ready):
                for m in range(KC):
                    for c in range(KC):
                        last = pe.matmul(dst[:, m * P:(m + 1) * P], w[:, c, m * P:(m + 1) * P], rhsT[:, c, :],
                                         start=(c == 0), stop=(c == KC - 1))
                last.then_inc(ready, 1)

            def proj_step(v):
                u = v.ahead(1)
                if u.real():
                    if u.static and u.t == 0:
                        pe.wait_ge(A_weights, 2 * KC)
                    pe.wait_ge(A_reluT, u.t + 1)
                    after(pe, A_copied, u.t - 1)
                    project(pq[:, u.parity, 0:D + 2], normedT[:, u.parity], w0, A_projected)
                u = v.ahead(3)
                if u.real():
                    pe.wait_ge(A_normed, u.t + 1)
                    after(pe, A_reluT, u.t - 1)
                    transposes(pt[:, u.parity, :], normed[:, u.parity, :], A_transposed)
                if v.real():
                    pe.wait_ge(A_scored, (v.t + 1) * 2)
                    after(pe, A_rowcopied, v.t - 1)
                    pe.matmul(pa[:, v.parity, 0:P], s2[:, v.parity:v.parity + 1].broadcast_to([P, P]), ident[:],
                              start=True, stop=True).then_inc(A_rowed, 1)
            pe.wait_ge(ident_made, 1)
            tile_loop(pe, proj_step, 3)

            def turn_targets(u):
                pe.wait_ge(Q_affine, (u.t + 1) * Q_AFFINES)
                transposes(pa[:, 0, 2 * P:4 * P], normed[:, u.parity, :], Q_T)

            def project_queries(u):
                pe.wait_ge(Q_Tcopied, u.t + 1)
                project_heads(pa[:, 1, 2 * P:4 * P], wq, normedT[:, 0], Q_proj)

            def gat_step(v):
                u = v.ahead(2)

                def turn(c):
                    if c == 0:
                        pe.wait_ge(B_probs, u.t + 1)
                    after(pe, B_evac, u.t * CH + c - 1)
                    for k in range(BLK):
                        last = pe.transpose(pt[:, c % 2, k * P:(k + 1) * P],
                                            scoresB[:, u.parity, (c * BLK + k) * P:(c * BLK + k + 1) * P], ident[:])
                    last.then_inc(B_T, 1)

                def weigh(c):
                    pe.wait_ge(B_evac, u.t * CH + c + 1)
                    if c == 0:
                        after(pe, B_step, (u.t - 2) * B_STEPS + 2)
                    for k in range(BLK):
                        last = pe.matmul(pa[:, u.parity, 0:D + 1], probsB[:, c, k * P:(k + 1) * P], hproj[:, c * BLK + k, :],
                                         start=(c + k == 0), stop=(c == CH - 1 and k == BLK - 1))
                    last.then_inc(B_av, 1)

                if u.real():
                    turn(0)
                    turn(1)
                    turn(2)
                    weigh(0)
                    turn(3)
                if v.real():
                    pe.wait_ge(B_affine, (v.t + 1) * B_AFFINES)
                    after(pe, B_hsTcopied, v.t)
                    transposes(pq[:, 0, 0:D], normed[:, v.parity, :], B_hsT)
                if u.real():
                    weigh(1)
                    weigh(2)
                if v.real():
                    pe.wait_ge(B_hsTcopied, v.t + 1)
                    after(pe, B_whole, v.t * KC)
                    project_heads(pq[:, 0, 512:512 + D], wk, normedT[:, 0], B_projK)
                    after(pe, B_vwhole, v.t)
                    project(pq[:, 1, 0:D], normedT[:, 0], wv, B_projV)
                if u.real():
                    weigh(3)
            pe.wait_ge(A_reluT, NT)
            pe.wait_ge(A_copied, NT)
            pe.wait_ge(A_rowcopied, NT)
            pe.wait_ge(ones_made, 3)
            pe.wait_ge(small_in, SMALL)
            turn_targets(Tile(0))
            project_queries(Tile(0))
            pe.wait_ge(Q_whole, KC)
            tile_loop(pe, gat_step, 3)

            def front(g):
                pe.wait_ge(ctx_rows_in, (g + 1) * 16)
                after(pe, D_step, g * D_STEPS)
                after(pe, D_postTcopied, g * GT)
                for k in range(GT + 1):
                    t = g * GT + k
                    if k < GT:
                        after(pe, D_ctxTcopied, t - 1)
                        transposes(pq[:, 0, (k % 2) * 512:(k % 2) * 512 + D], ctx_rows[:, k, :], D_ctxT)
                    if k:
                        pe.wait_ge(D_ctxTcopied, t)
                        project(pq[:, 1, (k - 1) * D:k * D], normedT[:, (k - 1) % 2], wo, D_attn)

            def turn_post(g, k):
                pe.wait_ge(D_post, g * GT + k + 1)
                after(pe, D_ctxTcopied, (g + 1) * GT)
                if k >= 2:
                    after(pe, D_postTcopied, g * GT + k - 1)
                transposes(pq[:, 0, (k % 2) * 512:(k % 2) * 512 + D], post[:, k, :], D_postT)

            def mha_step(v):
                for h in range(HEADS):
                    uq, hq, nq = unit(v, h + 4)
                    ua, ha, na = unit(v, h + 1)
                    n = v.t * HEADS + h

                    def weigh(c):
                        wait_parts(pe, ua, ha, c)
                        for k in range(BLK):
                            for part in (probs_a, probs_b):
                                last = pe.matmul(pa[0:VW, ha % 2, 0:P], value[:, c * BLK + k, ha, :], part[:, c, k * P:(k + 1) * P],
                                                 start=(c + k == 0 and part is probs_a),
                                                 stop=(c == CH - 1 and k == BLK - 1 and part is probs_b))
                        last.then_inc(C_av, 1)

                    if front_place(v, h):
                        pe.wait_ge(C_least, UNITS * 2)
                        pe.wait_ge(wo_in, 16)
                        front(0)
                    for half in range(2):
                        for c in (2 * half, 2 * half + 1):
                            ut, ht, ct, m = chunk_ahead(v, h, c)
                            if ut.real():
                                if ct % 2 == 0:
                                    pe.wait_ge(C_probs, (ut.t * HEADS + ht) * 2 + ct // 2 + 1)
                                wait_slot(pe, ut, ht, ct)
                                for k in range(BLK):
                                    last = pe.transpose(pt[:, ct % 2, k * P:(k + 1) * P],
                                                        ring[:, ht % 4, (ct * BLK + k) * P:(ct * BLK + k + 1) * P], ident[:])
                                last.then_inc(C_T, 1)
                        if v.real() and half == 1:
                            pe.wait_ge(C_contextT, n + 1)
                            pe.transpose(pa[:, h % 2, P:P + VW], contextT[:, h % 2, :], ident[0:VW, 0:VW]).then_inc(C_turned, 1)
                        if ua.real():
                            if half == 0:
                                after(pe, C_unscaled, na - 1)
                                if h == 1:
                                    pe.wait_ge(Q_Tcopied, queries_through(v))
                                if h == 2:
                                    pe.wait_ge(Q_whole, queries_through(v) * KC)
                            weigh(half * 2)
                            if not by_pool(ha, half * 2 + 1):
                                weigh(half * 2 + 1)
                        if uq.real():
                            if hq == 0 and half == 0:
                                pe.wait_ge(query_stacked[uq.parity], (uq.pair + 1) * 64)
                            if uq.static and nq == 0 and half == 1:
                                pe.wait_ge(key_stacked, NT * 64)
                            after(pe, C_least, nq * 2 + half - 1)
                            for k in range(2):
                                at = half * HALF + k * 512
                                last = pe.matmul(pq[:, half, k * 512:(k + 1) * 512], query_stack[:, uq.parity, hq, :],
                                                 key_stack[:, hq, at:at + 512], start=True, stop=True)
                            last.then_inc(C_qk, 1)
                        if ua.real() and by_pool(ha, half * 2 + 1):
                            weigh(half * 2 + 1)
                    u = v.ahead(1)
                    if later_tile(u) and v.real() and h < 2:
                        pe.wait_ge(C_unscaled, n + 1)
                    if later_tile(u) and h == 0:
                        turn_targets(u)
                    if later_tile(u) and h == 1:
                        project_queries(u)

            def queries_through(v):
                return min(v.t + 2, NT) if v.static else v.t + 2

            pe.wait_ge(B_hsTcopied, NT)
            pe.wait_ge(B_whole, NT * KC)
            pe.wait_ge(B_vwhole, NT)
            pe.wait_ge(B_parts, NT * B_PARTS)
            pe.wait_ge(B_evac, NT * CH)
            pe.wait_ge(B_step, NT * B_STEPS)
            pe.wait_ge(key_stacked, NT // 2 * 64)

            tile_loop(pe, mha_step, 2)

            def ffn_step(v):
                ahead = not isinstance(v, int) or v + 1 < NG
                if ahead:
                    front(v + 1)
                else:
                    pe.wait_ge(D_postTcopied, NT)
                for m in range(MC):
                    n = v * MC + m
                    if not (isinstance(n, int) and n < 2):
                        if m < 2:
                            after(pe, D_gelu, v * MC)
                        else:
                            after(pe, D_gelu, n - 1)
                    for c in range(KC):
                        last = pe.matmul(pt[:, m % 2, :], w1[:, c, m * P:(m + 1) * P], postT[:, c, :],
                                         start=(c == 0), stop=(c == KC - 1))
                    last.then_inc(D_hidden, 1)
                for k in range(GT):
                    if ahead:
                        turn_post(v + 1, k)
                    t = v * GT + k
                    if k < 2:
                        after(pe, D_out, v * GT)
                    else:
                        after(pe, D_out, t - 1)
                    for m in range(MC):
                        if k == 0:
                            pe.wait_ge(D_gelu, v * MC + m + 1)
                        last = pe.matmul(pa[:, k % 2, 0:D], hiddenT[:, m, k * P:(k + 1) * P], w2[:, m, :],
                                         start=(m == 0), stop=(m == MC - 1))
                    last.then_inc(D_ff, 1)
            for k in range(GT):
                turn_post(0, k)
            pe.wait_ge(C_unscaled, UNITS)
            pe.wait_ge(C_a, UNITS * CH)
            pe.wait_ge(C_b, UNITS * CH - UNITS // 2)
            pe.wait_ge(ffn_in, 32)
            group_loop(pe, ffn_step)

        @block.scalar
        def _(act):
            def proj_step(v):
                u = v.ahead(1)
                if u.real():
                    act.wait_ge(A_projected, u.t + 1)
                    after(act, A_rowed, u.t - 1)
                    act.copy(s1[:, bass.ds(u.t, 1)], pq[:, u.parity, D:D + 1]).then_inc(A_scored, 1)
                    act.copy(s2[:, u.parity:u.parity + 1], pq[:, u.parity, D + 1:D + 2]).then_inc(A_scored, 1)
                    act.copy(slot(hproj, u.t), pq[:, u.parity, 0:D]).then_inc(A_copied, 1)
                u = v.ahead(3)
                if u.real():
                    act.wait_ge(A_transposed, u.t + 1)
                    after(act, A_projected, u.t - 1)
                    act.activation(flat(normedT[:, u.parity]), pt[:, u.parity, 0:D], ACT.Relu).then_inc(A_reluT, 1)
                if v.real():
                    act.wait_ge(A_rowed, v.t + 1)
                    act.copy(src_row[:, cols(v.t)], pa[:, v.parity, 0:P]).then_inc(A_rowcopied, 1)
            tile_loop(act, proj_step, 3)

            def copy_targetsT(u):
                act.wait_ge(Q_T, u.t + 1)
                after(act, Q_proj, u.t)
                act.copy(flat(normedT[:, 0]), pa[:, 0, 2 * P:4 * P]).then_inc(Q_Tcopied, 1)

            def copy_queries(u):
                act.wait_ge(Q_proj, u.t + 1)
                after(act, Q_parts, u.t * Q_PARTS)
                for c in range(KC):
                    act.activation(whole[:, c, :], pa[:, 1, (2 + c) * P:(3 + c) * P], ACT.Identity, bias=bqc[:, c:c + 1],
                                   scale=-QSCALE).then_inc(Q_whole, 1)

            def gat_step(v):
                u = v.ahead(2)

                def evacuate(c):
                    act.wait_ge(B_T, u.t * CH + c + 1)
                    after(act, B_av, u.t * CH + c - 3)
                    act.copy(probsB[:, c, :], pt[:, c % 2, :]).then_inc(B_evac, 1)

                if u.real():
                    evacuate(0)
                    evacuate(1)
                    evacuate(2)
                e = v.ahead(1)
                if e.real():
                    act.wait_ge(B_step, e.t * B_STEPS + 3)
                    act.activation(row2[:], row2[:], ACT.Exp).then_inc(B_expneg, 1)
                if u.real():
                    evacuate(3)
                if v.real():
                    act.wait_ge(B_hsT, v.t + 1)
                    after(act, B_projV, v.t)
                    act.copy(flat(normedT[:, 0]), pq[:, 0, 0:D]).then_inc(B_hsTcopied, 1)
                w = v.ahead(4)
                if w.real():
                    after(act, B_T, (w.t - 1) * CH)
                    act.activation(scoresB[:, w.parity, :], src_row[:], ACT.Identity, bias=s1[:, bass.ds(w.t, 1)],
                                   scale=1.0).then_inc(B_scored, 1)
                    if w.static and w.t == 1:
                        copy_targetsT(Tile(0))
                        copy_queries(Tile(0))
                    if not (w.static and w.t == 0):
                        act.wait_ge(B_masked, w.t)
                        act.dma_start(adj_in[:], rows(adj, w.t)).then_inc(adjB_in, 16)
                w = v.ahead(3)
                if w.real():
                    act.wait_ge(B_least, w.t + 1)
                    act.activation(scoresB[:, w.parity, :], scoresB[:, w.parity, :], ACT.Exp, bias=least[:, w.parity, 1:2],
                                   scale=-1.0).then_inc(B_probs, 1)
                if v.real():
                    act.wait_ge(B_projK, v.t + 1)
                    if v.static and v.t == 0:
                        act.wait_ge(Q_parts, Q_PARTS)
                    after(act, B_parts, (v.t - 1) * B_PARTS + 2)
                    for c in range(KC):
                        act.activation(whole[:, c, :], pq[:, 0, 512 + c * P:512 + (c + 1) * P], ACT.Identity, bias=bkc[:, c:c + 1],
                                       scale=1.0).then_inc(B_whole, 1)
                    act.wait_ge(B_projV, v.t + 1)
                    after(act, B_parts, v.t * B_PARTS)
                    act.copy(vwhole[:], pq[:, 1, 0:D]).then_inc(B_vwhole, 1)
            act.wait_ge(A_rowcopied, NT)
            act.wait_ge(A_scored, NT * 2)
            act.wait_ge(A_projected, NT)
            act.wait_ge(small_in, SMALL)
            act.wait_ge(bq_scaled, 1)
            tile_loop(act, gat_step, 4)

            def mha_step(v):
                for h in range(HEADS):
                    ue, he, ne = unit(v, h + 3)
                    n = v.t * HEADS + h

                    def part_a_of(c):
                        ut, ht, ct, m = chunk_ahead(v, h, c)
                        if ut.real():
                            act.wait_ge(C_T, m + 1)
                            after(act, C_av, m - 3)
                            if by_pool(ht, ct):
                                after(act, C_pool_b, ut.t * (HEADS // 2) + ht // 2)
                                act.copy(raw[:], pt[:, ct % 2, :]).then_inc(C_raw, 1)
                            act.copy(probs_a[:, ct, :], pt[:, ct % 2, :]).then_inc(C_a, 1)

                    def exponentiate(half):
                        if ue.real():
                            if half == 0:
                                act.wait_ge(C_least, ne * 2 + 2)
                            here = ring[:, he % 4, half * HALF:(half + 1) * HALF]
                            act.activation(here, here, ACT.Exp, bias=least[:, he % 4, 1:2], scale=-1.0).then_inc(C_probs, 1)

                    if v.static and v.t == -1 and h == 4:
                        attention_over(act)
                    if front_place(v, h):
                        front(0)
                    part_a_of(0)
                    part_a_of(1)
                    if v.real():
                        act.wait_ge(C_av, (n + 1) * CH)
                        after(act, C_turned, n - 1)
                        act.copy(contextT[:, h % 2, :], pa[0:VW, h % 2, 0:P]).then_inc(C_contextT, 1)
                    exponentiate(0)
                    part_a_of(2)
                    part_a_of(3)
                    if v.real():
                        act.wait_ge(C_turned, n + 1)
                        if h == 0:
                            after(act, C_ctx, (v.t - 1) * 2)
                        act.copy(unscaled[:, v.parity, h, :], pa[:, h % 2, P:P + VW]).then_inc(C_unscaled, 1)
                    exponentiate(1)
                    u = v.ahead(1)
                    if later_tile(u) and h == 0:
                        copy_targetsT(u)
                    if later_tile(u) and h == 1:
                        copy_queries(u)
            def front(g):
                for k in range(GT):
                    t = g * GT + k
                    act.wait_ge(D_ctxT, t + 1)
                    after(act, D_attn, t - 1)
                    act.copy(flat(normedT[:, k % 2]), pq[:, 0, (k % 2) * 512:(k % 2) * 512 + D]).then_inc(D_ctxTcopied, 1)

            def copy_post(g):
                for k in range(GT):
                    act.wait_ge(D_postT, g * GT + k + 1)
                    after(act, D_hidden, g * MC)
                    act.copy(postT[:, :, k * P:(k + 1) * P],
                             pq[:, 0, (k % 2) * 512:(k % 2) * 512 + D].rearrange("p (c n) -> p c n", n=P)).then_inc(D_postTcopied, 1)

            act.wait_ge(B_parts, NT * B_PARTS)
            act.wait_ge(bq_scaled, 1)
            tile_loop(act, mha_step, 2)
            copy_post(0)

            def ffn_step(v):
                ahead = not isinstance(v, int) or v + 1 < NG
                if ahead:
                    front(v + 1)
                after(act, D_ff, v * GT)
                for m in range(MC):
                    act.wait_ge(D_hidden, v * MC + m + 1)
                    act.activation(hiddenT[:, m, :], pt[:, m % 2, :], ACT.Gelu_apprx_tanh).then_inc(D_gelu, 1)
                if ahead:
                    copy_post(v + 1)
            group_loop(act, ffn_step)

        @block.vector
        def _(dve):
            def proj_step(v):
                u = v.ahead(5)
                if u.real():
                    if u.static and u.t == 0:
                        dve.wait_ge(x_in[0], 16)
                    if u.static and u.t == GT:
                        for g in range(1, NG):
                            dve.wait_ge(x_in[g], 16)
                    row_stats(dve, Chain(dve, A_step, u.t * 3), slot(xres, u.t), u.parity)
                u = v.ahead(4)
                if u.real():
                    after(dve, A_transposed, u.t - 1)
                    normalise(dve, normed[:, u.parity, :], slot(xres, u.t), A_roots, u.t + 1, u.parity).then_inc(A_normed, 1)
                if u.static and u.t == 0:
                    dve.wait_ge(w0_in, 48)
                    for c in range(KC):
                        for i, junk in enumerate((row1, row2)):
                            after(dve, A_weights, c * 2)
                            dve.scalar_tensor_tensor(out=junk[:], in0=w0[:, c, 0:D], scalar=-1.0, in1=att[:, i, :], op0=ALU.mult,
                                                     op1=ALU.mult, accum_out=w0[:, c, D + i:D + i + 1]).then_inc(A_weights, 1)
            tile_loop(dve, proj_step, 5)

            def gat_step(v):
                e, w = v.ahead(1), v.ahead(3)
                chain = Chain(dve, B_step, e.t * B_STEPS)
                s = scoresB[:, w.parity, :]
                if e.real():
                    dve.wait_ge(B_av, (e.t + 1) * CH)
                    chain.link(dve.reciprocal(recip[:, 0:1], pa[:, e.parity, D:D + 1]))
                    chain.link(dve.tensor_scalar(row1[:], pa[:, e.parity, 0:D], recip[:, 0:1], None, ALU.mult))
                    chain.last(dve.tensor_scalar(row2[:], row1[:], 0.0, None, ALU.min))
                if w.real() and not (w.static and w.t == 0):
                    make_mask(w)
                if e.real():
                    dve.wait_ge(B_expneg, e.t + 1)
                    chain.link(dve.scalar_tensor_tensor(out=row1[:], in0=row2[:], scalar=-1.0, in1=row1[:], op0=ALU.add, op1=ALU.max))
                    chain.link(dve.tensor_tensor(slot(xres, e.t), slot(xres, e.t), row1[:], ALU.add), apart)
                    row_stats(dve, chain, slot(xres, e.t))
                if w.real():
                    apart(dve, (B_leaky, w.t + 1), (B_masked, w.t + 1))
                    dve.tensor_tensor_reduce(s, s, maskB[:], 1.0, HIGHEST, ALU.add, ALU.min,
                                             least[:, w.parity, 1:2]).then_inc(B_least, 1)
                if e.real():
                    chain.link(normalise(dve, row1[:], slot(xres, e.t), B_roots, e.t * 2 + 1))
                    chain.last(dve.tensor_scalar(row1[:], row1[:], 0.0, None, ALU.max))
                if e.real():
                    apart(dve, (B_step, e.t * B_STEPS + 10))
                    row_stats(dve, chain, row1[:])
                y = v.ahead(4)
                if y.real():
                    s = scoresB[:, y.parity, :]
                    dve.wait_ge(B_scored, y.t + 1)
                    dve.scalar_tensor_tensor(out=s, in0=s, scalar=ALPHA, in1=s, op0=ALU.mult, op1=ALU.min).then_inc(B_leaky, 1)
                if e.real():
                    after(dve, B_affine, e.t * B_AFFINES)
                    if e.static and e.t == 0:
                        dve.wait_ge(Q_affine, Q_AFFINES)
                    chain.last(normalise(dve, row3[:], row1[:], B_roots, e.t * 2 + 2))
                    assert chain.n == B_STEPS
            def target_stats(u):
                apart(dve, (target_in_sem[u.parity], (u.pair + 1) * 16))
                row_stats(dve, Chain(dve, Q_step, u.t * Q_STEPS), target_in[:, u.parity, :])

            def normalise_targets(u):
                after(dve, Q_affine, u.t * Q_AFFINES)
                normalise(dve, row3[:], target_in[:, u.parity, :], Q_roots, u.t + 1).then_inc(Q_step, 1)

            def make_mask(w):
                dve.wait_ge(adjB_in, (w.t + 1) * 16)
                after(dve, B_least, w.t)
                dve.tensor_scalar(maskB[:], adj_in[:], 0, MASKED, ALU.is_le, ALU.mult).then_inc(B_masked, 1)

            target_stats(Tile(0))
            make_mask(Tile(0))
            normalise_targets(Tile(0))
            tile_loop(dve, gat_step, 4)

            def mha_step(v):
                for h in range(HEADS):
                    def part_b_of(c):
                        ut, ht, ct, m = chunk_ahead(v, h, c)
                        if ut.real() and not by_pool(ht, ct):
                            dve.wait_ge(C_a, m + 1)
                            dve.tensor_tensor(probs_b[:, ct, :], pt[:, ct % 2, :], probs_a[:, ct, :].bitcast(F32),
                                              ALU.subtract).then_inc(C_b, 1)

                    def mask_and_least(ahead, half):
                        um, hm, nm = unit(v, h + ahead)
                        if um.real():
                            if hm == 0 and half == 0:
                                dve.wait_ge(C_masked, (um.t + 1) * PIECES)
                            apart(dve, (C_qk, nm * 2 + half + 1), (C_least, nm * 2 + half if half else 0))
                            at = slice(half * HALF, (half + 1) * HALF)
                            dve.tensor_tensor_reduce(ring[:, hm % 4, at], pq[:, half, :], mask[:, um.parity, at], 1.0,
                                                     least[:, hm % 4, 0:1] if half else HIGHEST, ALU.add, ALU.min,
                                                     least[:, hm % 4, half:half + 1]).then_inc(C_least, 1)

                    mask_and_least(3, 1)
                    part_b_of(0)
                    part_b_of(1)
                    mask_and_least(4, 0)
                    part_b_of(2)
                    part_b_of(3)
                    if front_place(v, h):
                        front_sums(0)
                    if front_place(v, h - 1):
                        front_rows(0)
                    u = v.ahead(2)
                    if later_tile(u) and h == 4:
                        target_stats(u)
                    if later_tile(u) and h == 6:
                        normalise_targets(u)
                if v.static and v.t == -2:
                    attention_over(dve)
                    dve.wait_ge(adjC_in, 16)
                    dve.tensor_scalar(mask[:, 0, :], adj_in[:], 0, MASKED, ALU.is_equal, ALU.mult).then_inc(C_masked, PIECES)
                if v.real():
                    here = unscaled[:, v.parity]
                    dve.wait_ge(C_unscaled, (v.t + 1) * HEADS)
                    after(dve, C_ctx, v.t * 2)
                    dve.reciprocal(recip[:, :].rearrange("p (h o) -> p h o", o=1), here[:, :, HD:HD + 1]).then_inc(C_recip, 1)
            def front_sums(g):
                base = g * D_STEPS
                dve.wait_ge(target_rows_in, (g + 1) * 16)
                dve.wait_ge(D_attn, (g + 1) * GT)
                after(dve, D_total, g * GT)
                dve.tensor_tensor(post[:], pq[:, 1, :].rearrange("p (k d) -> p k d", d=D),
                                  bor[:].rearrange("p (o d) -> p o d", o=1).broadcast_to([P, GT, D]), ALU.add).then_inc(D_step, 1)
                for k in range(GT):
                    dve.wait_ge(D_step, base + 1)
                    dve.scalar_tensor_tensor(out=target_rows[:, k, :], in0=post[:, k, :], scalar=node[:, bass.ds(g * GT + k, 1)],
                                             in1=target_rows[:, k, :], op0=ALU.mult, op1=ALU.add).then_inc(D_step, 1)
                for k in range(GT):
                    apart(dve, (D_step, base + k + 2))
                    dve.bn_stats(stats[:, k, :], target_rows[:, k, :]).then_inc(D_step, 1)
                for k in range(GT):
                    apart(dve, (D_step, base + GT + k + 2))
                    dve.bn_aggr(mv[:, k, :], stats[:, k, :]).then_inc(D_step, 1)
                dve.wait_ge(D_step, base + 3 * GT + 1)
                dve.tensor_scalar(mv[:, :, 1:2], mv[:, :, 1:2], EPS, None, ALU.add).then_inc(D_step, 1)

            def front_rows(g):
                base = g * D_STEPS + 3 * GT + 2
                for k in range(GT):
                    dve.scalar_tensor_tensor(out=target_rows[:, k, :], in0=target_rows[:, k, :], scalar=mv[:, k, 0:1], in1=ln2s[:],
                                             op0=ALU.subtract, op1=ALU.mult).then_inc(D_step, 1)
                dve.wait_ge(D_roots, g + 1)
                for k in range(GT):
                    dve.wait_ge(D_step, base + k + 1)
                    dve.scalar_tensor_tensor(out=target_rows[:, k, :], in0=target_rows[:, k, :], scalar=rstd[:, k:k + 1], in1=ln2b[:],
                                             op0=ALU.mult, op1=ALU.add).then_inc(D_step, 1)
                for k in range(GT):
                    dve.wait_ge(D_step, base + GT + k + 1)
                    dve.tensor_scalar(post[:, k, :], target_rows[:, k, :], node[:, bass.ds(g * GT + k, 1)], None, ALU.mult).then_inc(D_post, 1)
            tile_loop(dve, mha_step, 2)

            def ffn_step(v):
                if not isinstance(v, int) or v + 1 < NG:
                    front_sums(v + 1)
                    front_rows(v + 1)
                for k in range(GT):
                    t = v * GT + k
                    dve.wait_ge(D_ff, t + 1)
                    dve.wait_ge(D_total, t + 1)
                    dve.tensor_tensor(slot(total, t), slot(total, t), pa[:, k % 2, 0:D], ALU.add).then_inc(D_out, 1)
            group_loop(dve, ffn_step)


_INS = ["x", "adj", "nodemask", "L0_gnn_W", "L0_gnn_attn", "L1_gnn_h_target", "L1_gnn_ln1_scale", "L1_gnn_ln1_bias",
        "L1_gnn_Wq", "L1_gnn_bq", "L1_gnn_Wk", "L1_gnn_bk", "L1_gnn_Wv", "L1_gnn_bv", "L1_gnn_Wo", "L1_gnn_bo",
        "L1_gnn_ln2_scale", "L1_gnn_ln2_bias", "L1_gnn_W1", "L1_gnn_W2"]


def kernel(**inputs):
    import numpy as np
    import concourse.bacc as bacc
    from concourse.bass_utils import run_bass_kernel_spmd

    nc = bacc.Bacc("TRN2", target_bir_lowering=False, num_devices=1)
    arrays, args = {}, []
    for name in _INS:
        a = np.ascontiguousarray(inputs[name])
        arrays[f"in_{name}"] = a
        args.append(nc.dram_tensor(f"in_{name}", a.shape, mybir.dt.from_np(a.dtype), kind="ExternalInput").ap())
    args.append(nc.dram_tensor("out_x", (N, D), F32, kind="ExternalOutput").ap())
    build(nc, *args)
    r = run_bass_kernel_spmd(nc, [arrays], core_ids=[0])
    return r.results[0]["out_x"]
```
